# Optimizing a Trainium2 kernel written in Bass

```python
import numpy as np
import jax
import jax.numpy as jnp

def _softmax(x, axis=-1):
    return jax.nn.softmax(x, axis=axis)

def _gelu(x):
    return jax.nn.gelu(x, approximate=True)

def _silu(x):
    return jax.nn.silu(x)

def _sigmoid(x):
    return jax.nn.sigmoid(x)

def _layernorm(x, axis=-1, eps=1e-05):
    m = jnp.mean(x, axis=axis, keepdims=True)
    v = jnp.var(x, axis=axis, keepdims=True)
    return (x - m) / jnp.sqrt(v + eps)

def _scatter_add(tgt, idx, src, axis=0):
    return tgt.at[idx].add(src)

def _segment_sum(src, seg, n):
    return jax.ops.segment_sum(src, seg, n)
kernel_name = 'mk_flamingo_gated_d2_seqx_r4_53d749'

def setup_inputs(seed: int=0):
    np.random.seed(seed)
    _w = jnp.asarray

    def _rec_inputs():
        import jax
        import jax.numpy as jnp
        _rk = jax.random.key(seed)
        x = -0.0002928 + 1 * jax.random.normal(jax.random.fold_in(_rk, 1), (16, 512, 256), jnp.float32)
        _lenS = 512 - jax.random.randint(jax.random.fold_in(_rk, 7), (16,), 0, max(1, 512 // 4) + 1, jnp.int32)
        _lenS2 = 64 - jax.random.randint(jax.random.fold_in(_rk, 8), (16,), 0, max(1, 64 // 4) + 1, jnp.int32)
        _ctx_512P = jax.random.normal(jax.random.fold_in(_rk, 11), (16, 16, 128), jnp.float32)
        _ctx_512c = jax.random.dirichlet(jax.random.fold_in(_rk, 511), 0.3 * jnp.ones((16,), jnp.float32), (16, 64))
        _ctx_512t = jnp.einsum('bsk,bkd->bsd', _ctx_512c, _ctx_512P)
        _ctx_512t = _ctx_512t * jax.lax.rsqrt(jnp.mean(jnp.square(_ctx_512t)) + 1e-12) * 0.953939
        ctx_512 = 0.00222621 + 0.99962 * (_ctx_512t + 0.3 * jax.random.normal(jax.random.fold_in(_rk, 611), (16, 64, 128), jnp.float32))
        _g = jax.random.normal(jax.random.fold_in(_rk, 9001), (2, 2), jnp.float32)
        _g = jnp.sign(_g) * jnp.maximum(jnp.abs(_g), 1.0) + (_g == 0) * 1.0
        g_xattn = _g[0]
        g_ffn = _g[1]
        return (x, ctx_512, g_xattn, g_ffn)
    x, ctx_512, g_xattn, g_ffn = _rec_inputs()

    def _L0_xattn_setup():
        import jax, jax.numpy as jnp
        import numpy as np
        B, T, TC, C, CC, H = (2, 512, 128, 256, 128, 16)
        D = C // H

        def _heads(t):
            b, l, _ = t.shape
            return t.reshape(b, l, H, D).transpose(0, 2, 1, 3)
        key = jax.random.key(seed)
        ks = jax.random.split(key, 18)
        w = lambda k, i, o: jax.random.normal(k, (i, o), jnp.float32) / np.sqrt(i).astype(np.float32)
        return {'x': jax.random.normal(ks[0], (B, T, C), jnp.float32), 'cross_input': jax.random.normal(ks[1], (B, TC, CC), jnp.float32), 'Wk': w(ks[2], C, C), 'bk': jnp.zeros((C,), jnp.float32), 'Wq': w(ks[3], C, C), 'bq': jnp.zeros((C,), jnp.float32), 'Wv': w(ks[4], C, C), 'bv': jnp.zeros((C,), jnp.float32), 'Wck': w(ks[5], CC, C), 'bck': jnp.zeros((C,), jnp.float32), 'Wcq': w(ks[6], C, C), 'bcq': jnp.zeros((C,), jnp.float32), 'Wcv': w(ks[7], CC, C), 'bcv': jnp.zeros((C,), jnp.float32), 'Wp': w(ks[8], C, C), 'bp': jnp.zeros((C,), jnp.float32)}
    _L0_xattn_all = _L0_xattn_setup()
    _L0_xattn_in = {k: v for k, v in _L0_xattn_all.items() if k in ('Wk', 'bk', 'Wq', 'bq', 'Wv', 'bv', 'Wck', 'bck', 'Wcq', 'bcq', 'Wcv', 'bcv', 'Wp', 'bp')}
    del _L0_xattn_all

    def _L0_ffn_setup():
        import jax, jax.numpy as jnp
        import numpy as np
        H = 256
        I = 512
        E = 32
        B, S = (4, 512)

        def _grouped_mm(a, w, group_sizes):
            return jax.lax.ragged_dot(a, w, group_sizes)

        def _swiglu(x, gw, uw, dw):
            return jax.nn.silu(x @ gw) * (x @ uw) @ dw
        key = jax.random.key(seed)
        ks = jax.random.split(key, 8)
        scale = 0.02
        inp = {'hidden_states': jax.random.normal(ks[0], (B, S, H), dtype=jnp.float32), 'gate_w': jax.random.normal(ks[1], (H, E), dtype=jnp.float32) * scale, 'shared_gate_w': jax.random.normal(ks[2], (H, I), dtype=jnp.float32) * scale, 'shared_up_w': jax.random.normal(ks[3], (H, I), dtype=jnp.float32) * scale, 'shared_down_w': jax.random.normal(ks[4], (I, H), dtype=jnp.float32) * scale, 'routed_gate_w': jax.random.normal(ks[5], (E, H, I), dtype=jnp.float32) * scale, 'routed_up_w': jax.random.normal(ks[6], (E, H, I), dtype=jnp.float32) * scale, 'routed_down_w': jax.random.normal(ks[7], (E, I, H), dtype=jnp.float32) * scale}
        return inp
    _L0_ffn_all = _L0_ffn_setup()
    _L0_ffn_in = {k: v for k, v in _L0_ffn_all.items() if k in ('gate_w', 'shared_gate_w', 'shared_up_w', 'shared_down_w', 'routed_gate_w', 'routed_up_w', 'routed_down_w')}
    del _L0_ffn_all

    def _L1_xattn_setup():
        import jax, jax.numpy as jnp
        import numpy as np
        HEADS = 16
        D_MODEL = 256
        IMG_MODEL = 128
        D_K = D_MODEL // HEADS
        key = jax.random.key(seed)
        ks = jax.random.split(key, 12)
        B, LQ, LKV = (8, 512, 256)
        s_dm = 1.0 / np.sqrt(D_MODEL)
        s_im = 1.0 / np.sqrt(IMG_MODEL)
        return {'q': jax.random.normal(ks[0], (B, LQ, D_MODEL), jnp.float32), 'k': jax.random.normal(ks[1], (B, LKV, IMG_MODEL), jnp.float32), 'v': jax.random.normal(ks[2], (B, LKV, IMG_MODEL), jnp.float32), 'Wq': jax.random.normal(ks[3], (D_MODEL, D_MODEL), jnp.float32) * s_dm, 'bq': jnp.zeros((D_MODEL,), jnp.float32), 'Wk': jax.random.normal(ks[4], (IMG_MODEL, D_MODEL), jnp.float32) * s_im, 'bk': jnp.zeros((D_MODEL,), jnp.float32), 'Wv': jax.random.normal(ks[5], (IMG_MODEL, D_MODEL), jnp.float32) * s_im, 'bv': jnp.zeros((D_MODEL,), jnp.float32), 'Wo': jax.random.normal(ks[6], (D_MODEL, D_MODEL), jnp.float32) * s_dm, 'bo': jnp.zeros((D_MODEL,), jnp.float32)}
    _L1_xattn_all = _L1_xattn_setup()
    _L1_xattn_in = {k: v for k, v in _L1_xattn_all.items() if k in ('Wq', 'bq', 'Wk', 'bk', 'Wv', 'bv', 'Wo', 'bo')}
    del _L1_xattn_all

    def _L1_ffn_setup():
        import jax, jax.numpy as jnp
        import numpy as np
        D_IN, D_HID = (256, 1024)

        def _ternary(key, shape):
            return jax.random.randint(key, shape, -1, 2).astype(jnp.float32)

        def _tlin(x, w, s):
            return jnp.einsum('bsi,oi->bso', x, w) * s
        key = jax.random.key(seed)
        ks = jax.random.split(key, 12)
        inv = lambda fan: 1.0 / np.sqrt(fan).astype(np.float32)
        return {'x': jax.random.normal(ks[0], (4, 512, D_IN), dtype=jnp.float32), 'w1_w': _ternary(ks[1], (D_HID, D_IN)), 'w1_s': jax.random.uniform(ks[2], (D_HID,), dtype=jnp.float32) * inv(D_IN), 'w2_w': _ternary(ks[3], (D_HID, D_IN)), 'w2_s': jax.random.uniform(ks[4], (D_HID,), dtype=jnp.float32) * inv(D_IN), 'h1_w': _ternary(ks[5], (D_HID, D_HID)), 'h1_s': jax.random.uniform(ks[6], (D_HID,), dtype=jnp.float32) * inv(D_HID), 'h2_w': _ternary(ks[7], (D_HID, D_HID)), 'h2_s': jax.random.uniform(ks[8], (D_HID,), dtype=jnp.float32) * inv(D_HID), 'w3_w': _ternary(ks[9], (D_IN, D_HID)), 'w3_s': jax.random.uniform(ks[10], (D_IN,), dtype=jnp.float32) * inv(D_HID)}
    _L1_ffn_all = _L1_ffn_setup()
    _L1_ffn_in = {k: v for k, v in _L1_ffn_all.items() if k in ('w1_w', 'w1_s', 'w2_w', 'w2_s', 'h1_w', 'h1_s', 'h2_w', 'h2_s', 'w3_w', 'w3_s')}
    del _L1_ffn_all
    return {'x': x, 'ctx_512': ctx_512, 'g_xattn': g_xattn, 'g_ffn': g_ffn, 'L0_xattn_Wk': _L0_xattn_in['Wk'], 'L0_xattn_bk': _L0_xattn_in['bk'], 'L0_xattn_Wq': _L0_xattn_in['Wq'], 'L0_xattn_bq': _L0_xattn_in['bq'], 'L0_xattn_Wv': _L0_xattn_in['Wv'], 'L0_xattn_bv': _L0_xattn_in['bv'], 'L0_xattn_Wck': _L0_xattn_in['Wck'], 'L0_xattn_bck': _L0_xattn_in['bck'], 'L0_xattn_Wcq': _L0_xattn_in['Wcq'], 'L0_xattn_bcq': _L0_xattn_in['bcq'], 'L0_xattn_Wcv': _L0_xattn_in['Wcv'], 'L0_xattn_bcv': _L0_xattn_in['bcv'], 'L0_xattn_Wp': _L0_xattn_in['Wp'], 'L0_xattn_bp': _L0_xattn_in['bp'], 'L0_ffn_gate_w': _L0_ffn_in['gate_w'], 'L0_ffn_shared_gate_w': _L0_ffn_in['shared_gate_w'], 'L0_ffn_shared_up_w': _L0_ffn_in['shared_up_w'], 'L0_ffn_shared_down_w': _L0_ffn_in['shared_down_w'], 'L0_ffn_routed_gate_w': _L0_ffn_in['routed_gate_w'], 'L0_ffn_routed_up_w': _L0_ffn_in['routed_up_w'], 'L0_ffn_routed_down_w': _L0_ffn_in['routed_down_w'], 'L1_xattn_Wq': _L1_xattn_in['Wq'], 'L1_xattn_bq': _L1_xattn_in['bq'], 'L1_xattn_Wk': _L1_xattn_in['Wk'], 'L1_xattn_bk': _L1_xattn_in['bk'], 'L1_xattn_Wv': _L1_xattn_in['Wv'], 'L1_xattn_bv': _L1_xattn_in['bv'], 'L1_xattn_Wo': _L1_xattn_in['Wo'], 'L1_xattn_bo': _L1_xattn_in['bo'], 'L1_ffn_w1_w': _L1_ffn_in['w1_w'], 'L1_ffn_w1_s': _L1_ffn_in['w1_s'], 'L1_ffn_w2_w': _L1_ffn_in['w2_w'], 'L1_ffn_w2_s': _L1_ffn_in['w2_s'], 'L1_ffn_h1_w': _L1_ffn_in['h1_w'], 'L1_ffn_h1_s': _L1_ffn_in['h1_s'], 'L1_ffn_h2_w': _L1_ffn_in['h2_w'], 'L1_ffn_h2_s': _L1_ffn_in['h2_s'], 'L1_ffn_w3_w': _L1_ffn_in['w3_w'], 'L1_ffn_w3_s': _L1_ffn_in['w3_s']}

def reference(x, ctx_512, g_xattn, g_ffn, L0_xattn_Wk, L0_xattn_bk, L0_xattn_Wq, L0_xattn_bq, L0_xattn_Wv, L0_xattn_bv, L0_xattn_Wck, L0_xattn_bck, L0_xattn_Wcq, L0_xattn_bcq, L0_xattn_Wcv, L0_xattn_bcv, L0_xattn_Wp, L0_xattn_bp, L0_ffn_gate_w, L0_ffn_shared_gate_w, L0_ffn_shared_up_w, L0_ffn_shared_down_w, L0_ffn_routed_gate_w, L0_ffn_routed_up_w, L0_ffn_routed_down_w, L1_xattn_Wq, L1_xattn_bq, L1_xattn_Wk, L1_xattn_bk, L1_xattn_Wv, L1_xattn_bv, L1_xattn_Wo, L1_xattn_bo, L1_ffn_w1_w, L1_ffn_w1_s, L1_ffn_w2_w, L1_ffn_w2_s, L1_ffn_h1_w, L1_ffn_h1_s, L1_ffn_h2_w, L1_ffn_h2_s, L1_ffn_w3_w, L1_ffn_w3_s):
    import jax
    import jax.numpy as jnp

    def _L0_xattn_ref(x, cross_input, Wk, bk, Wq, bq, Wv, bv, Wck, bck, Wcq, bcq, Wcv, bcv, Wp, bp):
        import jax, jax.numpy as jnp
        import numpy as np
        B, T, TC, C, CC, H = (2, 512, 128, 256, 128, 16)
        D = C // H

        def _heads(t):
            b, l, _ = t.shape
            return t.reshape(b, l, H, D).transpose(0, 2, 1, 3)
        scale = np.float32(1.0 / np.sqrt(D))
        q = _heads(x @ Wq + bq)
        k = _heads(x @ Wk + bk)
        v = _heads(x @ Wv + bv)
        att = jnp.einsum('bhqd,bhkd->bhqk', q, k) * scale
        causal = jnp.tril(jnp.ones((T, T), bool))
        att = jnp.where(causal[None, None], att, -jnp.inf)
        y = jnp.einsum('bhqk,bhkd->bhqd', jax.nn.softmax(att, axis=-1), v)
        qc = _heads(x @ Wcq + bcq)
        kc = _heads(cross_input @ Wck + bck)
        vc = _heads(cross_input @ Wcv + bcv)
        attc = jnp.einsum('bhqd,bhkd->bhqk', qc, kc) * scale
        y = y + jnp.einsum('bhqk,bhkd->bhqd', jax.nn.softmax(attc, axis=-1), vc)
        y = y.transpose(0, 2, 1, 3).reshape(x.shape[0], T, C)
        return y @ Wp + bp

    def _L0_ffn_ref(hidden_states, gate_w, shared_gate_w, shared_up_w, shared_down_w, routed_gate_w, routed_up_w, routed_down_w):
        import jax, jax.numpy as jnp
        import numpy as np
        H = 256
        I = 512
        E = 32
        B, S = (4, 512)

        def _grouped_mm(a, w, group_sizes):
            return jax.lax.ragged_dot(a, w, group_sizes)

        def _swiglu(x, gw, uw, dw):
            return jax.nn.silu(x @ gw) * (x @ uw) @ dw
        b, s, h = hidden_states.shape
        x = hidden_states.reshape(-1, h)
        shared_out = _swiglu(x, shared_gate_w, shared_up_w, shared_down_w)
        logits = x @ gate_w
        topk_ids = jnp.argmax(logits, axis=-1)
        topk_val = jnp.max(logits, axis=-1)
        scores = jax.nn.sigmoid(topk_val)[:, None]
        xs = x * scores
        tokens_per_expert = jnp.zeros((E,), jnp.int32).at[topk_ids].add(1)
        order = jnp.argsort(topk_ids)
        sorted_x = xs[order]
        g = _grouped_mm(sorted_x, routed_gate_w, tokens_per_expert)
        u = _grouped_mm(sorted_x, routed_up_w, tokens_per_expert)
        d = _grouped_mm(jax.nn.silu(g) * u, routed_down_w, tokens_per_expert)
        inv = jnp.argsort(order)
        routed_out = d[inv]
        return (shared_out + routed_out).reshape(b, s, h)

    def _L1_xattn_ref(q, k, v, Wq, bq, Wk, bk, Wv, bv, Wo, bo):
        import jax, jax.numpy as jnp
        import numpy as np
        HEADS = 16
        D_MODEL = 256
        IMG_MODEL = 128
        D_K = D_MODEL // HEADS
        B, LQ, _ = q.shape
        LKV = k.shape[1]
        qh = (q @ Wq + bq).reshape(B, LQ, HEADS, D_K).transpose(0, 2, 1, 3)
        kh = (k @ Wk + bk).reshape(B, LKV, HEADS, D_K).transpose(0, 2, 1, 3)
        vh = (v @ Wv + bv).reshape(B, LKV, HEADS, D_K).transpose(0, 2, 1, 3)
        scale = 1.0 / np.sqrt(D_K)
        scores = jnp.einsum('bhqd,bhkd->bhqk', qh, kh) * scale
        attn = jax.nn.softmax(scores, axis=-1)
        out = jnp.einsum('bhqk,bhkd->bhqd', attn, vh)
        concat = out.transpose(0, 2, 1, 3).reshape(B, LQ, D_MODEL)
        return concat @ Wo + bo

    def _L1_ffn_ref(x, w1_w, w1_s, w2_w, w2_s, h1_w, h1_s, h2_w, h2_s, w3_w, w3_s):
        import jax, jax.numpy as jnp
        import numpy as np
        D_IN, D_HID = (256, 1024)

        def _ternary(key, shape):
            return jax.random.randint(key, shape, -1, 2).astype(jnp.float32)

        def _tlin(x, w, s):
            return jnp.einsum('bsi,oi->bso', x, w) * s
        h = jax.nn.silu(_tlin(x, w1_w, w1_s)) * _tlin(x, w2_w, w2_s)
        h = jax.nn.gelu(_tlin(h, h1_w, h1_s), approximate=False)
        h = jax.nn.gelu(_tlin(h, h2_w, h2_s), approximate=False)
        return _tlin(h, w3_w, w3_s)
    x = x + jnp.tanh(g_xattn[0]) * _L0_xattn_ref(_layernorm(x, axis=-1), ctx_512, L0_xattn_Wk, L0_xattn_bk, L0_xattn_Wq, L0_xattn_bq, L0_xattn_Wv, L0_xattn_bv, L0_xattn_Wck, L0_xattn_bck, L0_xattn_Wcq, L0_xattn_bcq, L0_xattn_Wcv, L0_xattn_bcv, L0_xattn_Wp, L0_xattn_bp)
    x = x + jnp.tanh(g_ffn[0]) * _L0_ffn_ref(_layernorm(x, axis=-1), L0_ffn_gate_w, L0_ffn_shared_gate_w, L0_ffn_shared_up_w, L0_ffn_shared_down_w, L0_ffn_routed_gate_w, L0_ffn_routed_up_w, L0_ffn_routed_down_w)
    x = x + jnp.tanh(g_xattn[1]) * _L1_xattn_ref(_layernorm(x, axis=-1), ctx_512, ctx_512, L1_xattn_Wq, L1_xattn_bq, L1_xattn_Wk, L1_xattn_bk, L1_xattn_Wv, L1_xattn_bv, L1_xattn_Wo, L1_xattn_bo)
    x = x + jnp.tanh(g_ffn[1]) * _L1_ffn_ref(_layernorm(x, axis=-1), L1_ffn_w1_w, L1_ffn_w1_s, L1_ffn_w2_w, L1_ffn_w2_s, L1_ffn_h1_w, L1_ffn_h1_s, L1_ffn_h2_w, L1_ffn_h2_s, L1_ffn_w3_w, L1_ffn_w3_s)
    return x

_drawn_inputs = setup_inputs


def setup_inputs(seed=0):
    import zlib

    import numpy as np

    out = dict(_drawn_inputs(seed))
    spreads = {'g_ffn': (-1.0, 0.2),
     'L0_xattn_bk': (0.0, 0.1),
     'L0_xattn_bq': (0.0, 0.1),
     'L0_xattn_bv': (0.0, 0.1),
     'L0_xattn_bck': (0.0, 0.1),
     'L0_xattn_bcq': (0.0, 0.1),
     'L0_xattn_bcv': (0.0, 0.1),
     'L0_xattn_bp': (0.0, 0.1),
     'L1_xattn_bq': (0.0, 0.1),
     'L1_xattn_bk': (0.0, 0.1),
     'L1_xattn_bv': (0.0, 0.1),
     'L1_xattn_bo': (0.0, 0.1)}
    factors = {}
    for name, (base, spread) in spreads.items():
        noise = np.random.default_rng([zlib.crc32(name.encode()), seed]).standard_normal(out[name].shape)
        drawn = base * np.exp(spread * noise) if base else spread * noise
        out[name] = jnp.asarray(drawn.astype(out[name].dtype))
    for name, factor in factors.items():
        out[name] = (out[name] * factor).astype(out[name].dtype)
    return out
```

```python
from contextlib import ExitStack

import concourse.bass as bass
import concourse.mybir as mybir

F32 = mybir.dt.float32
F32R = mybir.dt.float32r
BF16 = mybir.dt.bfloat16
I32 = mybir.dt.int32
ALU = mybir.AluOpType
ACT = mybir.ActivationFunctionType
AXIS = mybir.AxisListType.X

P = 128
B, T, C = 16, 512, 256
TC, CC = 64, 128
H, DH = 16, 16
E, HID = 32, 512
DH1 = 1024
NT = T // P
CK = C // P
QUADS = H // 4
NTILES = B * NT
SLOTS = NTILES + E - 1
HK = HID // P
DK = DH1 // P
EPS = 1e-5
SCALE = 1.0 / DH ** 0.5
MASKED = -1e30
ROWS = 4 * DH
KROWS = ROWS + 2
VW = 32


def flat(marks):
    for m in marks:
        if m is None:
            continue
        if isinstance(m, list):
            yield from flat(m)
        else:
            yield m


class Engine:

    def __init__(self, nc, queue, name, serial=False):
        self.q, self.name, self.serial = queue, name, serial
        self.sem = nc.alloc_semaphore(f"{name}_done")
        self.count = 0
        self.waited = {}

    def mark(self, instruction):
        instruction.then_inc(self.sem, 1)
        self.count += 1
        if self.serial:
            self.need((self.sem, self.count))
        return (self.sem, self.count)

    def need(self, *marks):
        for sem, value in flat(marks):
            if self.waited.get(sem.name, 0) < value:
                self.waited[sem.name] = value
                self.q.wait_ge(sem, value)


class Stream:

    def __init__(self, nc, name):
        self.sem = nc.alloc_semaphore(f"{name}_dma")
        self.count = 0

    def start(self, engine, out, in_, **how):
        engine.q.dma_start(out, in_, **how).then_inc(self.sem, 16)
        self.count += 16
        return (self.sem, self.count)

    def last(self):
        return (self.sem, self.count)


class Slot:
    def __init__(self, ap, index):
        self.ap, self.index, self.free, self.held = ap, index, None, False


class Ring:

    def __init__(self, aps):
        self.slots = [Slot(a, i) for i, a in enumerate(aps)]
        self.n = 0

    def take(self):
        s = self.slots[self.n % len(self.slots)]
        assert not s.held
        s.held = True
        self.n += 1
        return s


def release(slot, *marks):
    slot.free = list(marks)
    slot.held = False


class Plan:

    def __init__(self):
        self.waiting = []

    def add(self, start, span, steps, generator):
        self.waiting.append([start, len(self.waiting), span / steps, generator])

    def run(self):
        while self.waiting:
            entry = min(self.waiting, key=lambda e: e[:2])
            for _ in entry[3]:
                entry[0] += entry[2]
                break
            else:
                self.waiting.remove(entry)


class Temporary(ExitStack):
    pass


class Program:
    def __init__(self, nc, inp, out):
        self.nc, self.inp, self.out = nc, inp, out
        self.pe = Engine(nc, nc.tensor, "pe")
        self.act = Engine(nc, nc.scalar, "act")
        self.dve = Engine(nc, nc.vector, "dve")
        self.pool = Engine(nc, nc.gpsimd, "pool", serial=True)
        self.sp = Engine(nc, nc.sync, "sp")
        self.engines = [self.pe, self.act, self.dve, self.pool, self.sp]
        self.streams = {}
        self.x1 = nc.dram_tensor("x_after_attention0", [B, T, C], F32).ap()
        self.x2 = nc.dram_tensor("x_after_shared0", [B, T, C], F32).ap()
        self.x3 = nc.dram_tensor("x_after_attention1", [B, T, C], F32).ap()
        self.sorted_x = nc.dram_tensor("sorted_x", [SLOTS * P, C], F32).ap()
        self.sorted_y = nc.dram_tensor("sorted_y", [SLOTS * P, C], F32).ap()
        self.psum = nc.alloc_psum_tensor("psum", [P, 8 * 512], F32).ap()

    def stream(self, name):
        if name not in self.streams:
            self.streams[name] = Stream(self.nc, name)
        return self.streams[name]

    def bank(self, i, n=1):
        return self.psum[:, i * 512:(i + n) * 512]

    def sb(self, scope, name, shape, dt=F32):
        side = "right" if isinstance(scope, Temporary) else "left"
        return scope.enter_context(self.nc.sbuf_tensor(name, shape, dt, side=side)).ap()

    def sbs(self, scope, name, n, shape, dt=F32):
        return [self.sb(scope, f"{name}{i}", shape, dt) for i in range(n)]

    def barrier(self):
        marks = [(e.sem, e.count) for e in self.engines if e.count] + [s.last() for s in self.streams.values()]
        for e in self.engines:
            e.need(marks)

    def split_psum(self, src, hi, lo, needs, free, bias=None):
        self.act.need(needs, free)
        if bias is None:
            m_hi = self.act.mark(self.nc.scalar.activation(hi, src, ACT.Copy))
        else:
            m_hi = self.act.mark(self.nc.scalar.activation(hi, src, ACT.Identity, bias=bias))
        self.dve.need(m_hi, free)
        if bias is None:
            m_lo = self.dve.mark(self.nc.vector.tensor_tensor(lo, src, hi.bitcast(F32), ALU.subtract))
        else:
            m_lo = self.dve.mark(self.nc.vector.scalar_tensor_tensor(
                out=lo, in0=src, scalar=bias, in1=hi.bitcast(F32), op0=ALU.add, op1=ALU.subtract))
        return [m_hi, m_lo]

    def split_sbuf(self, src, hi, lo, needs):
        self.dve.need(needs)
        m = self.dve.mark(self.nc.vector.tensor_copy(hi, src))
        self.dve.need(m)
        return self.dve.mark(self.nc.vector.tensor_tensor(lo, src, hi.bitcast(F32), ALU.subtract))

    def product(self, out, pairs, start=True, stop=True, **how):
        for n, (lhsT, rhs) in enumerate(pairs):
            last = self.nc.tensor.matmul(out, lhsT, rhs, start=start and n == 0, stop=stop and n == len(pairs) - 1, **how)
        return last

    def constants(self, scope):
        nc, pool, dve, act = self.nc, self.pool, self.dve, self.act
        self.ident = self.sb(scope, "ident", [P, P])
        self.ident16 = self.sb(scope, "ident16", [P, P], BF16)
        self.mask_qk = self.sb(scope, "mask_qk", [P, P], BF16)
        self.mask_kq = self.sb(scope, "mask_kq", [P, P], BF16)
        self.before = self.sb(scope, "before", [P, P], BF16)
        self.ones16 = self.sb(scope, "ones16", [P, P], BF16)
        self.ones = self.sb(scope, "ones", [P, P])
        self.half = self.sb(scope, "minus_half", [P, NT])
        self.gate = self.sb(scope, "gate", [P, 4])
        for t, v in ((self.ident, 0.0), (self.ident16, 0.0), (self.mask_qk, 0.0), (self.mask_kq, 0.0),
                     (self.before, 0.0), (self.ones16, 1.0), (self.ones, 1.0), (self.half, -0.5)):
            m = pool.mark(nc.gpsimd.memset(t, v))
        pool.need(m)

        def select(t, op, fill, step, per_partition):
            nc_i = nc.gpsimd.affine_select(out=t, in_=t, compare_op=op, fill=fill, base=0,
                                           pattern=[[step, P]], channel_multiplier=per_partition)
            return pool.mark(nc_i)
        select(self.ident, ALU.not_equal, 1.0, -1, 1)
        select(self.ident16, ALU.not_equal, 1.0, -1, 1)
        select(self.mask_qk, ALU.is_ge, MASKED, -1, 1)
        select(self.mask_kq, ALU.is_ge, MASKED, 1, -1)
        made = select(self.before, ALU.is_ge, 1.0, -1, 1)
        raw = self.sb(scope, "gate_raw", [P, 4])
        s = self.stream("setup")
        s.start(self.sp, raw[:, 0:2], self.inp["g_xattn"].partition_broadcast(P))
        m = s.start(self.sp, raw[:, 2:4], self.inp["g_ffn"].partition_broadcast(P))
        act.need(m)
        m = act.mark(nc.scalar.activation(self.gate, raw, ACT.Tanh))
        for e in (self.pe, self.dve, self.act, self.pool, self.sp):
            e.need(made, m)

    def norm(self, x, y, stats, needs, free):
        nc, dve, pool = self.nc, self.dve, self.pool
        dve.need(needs, free)
        for t in range(NT):
            m = dve.mark(nc.vector.bn_stats(stats["raw"][:, t, :], x[:, t, :]))
        dve.need(m)
        for t in range(NT):
            m = dve.mark(nc.vector.bn_aggr(stats["mv"][:, t, :], stats["raw"][:, t, :]))
        dve.need(m)
        m = dve.mark(nc.vector.tensor_scalar(stats["var"], stats["mv"][:, :, 1], EPS, None, ALU.add))
        pool.need(m)
        m = pool.mark(nc.gpsimd.tensor_tensor(stats["rstd"], stats["var"], self.half, ALU.pow))
        dve.need(m)
        for t in range(NT):
            m = dve.mark(nc.vector.tensor_scalar(y[:, t, :], x[:, t, :], stats["mv"][:, t, 0:1],
                                                 stats["rstd"][:, t:t + 1], ALU.subtract, ALU.mult))
        return m

    def norm_scratch(self, scope, name):
        return {"raw": self.sb(scope, f"{name}_raw", [P, NT, 6]), "mv": self.sb(scope, f"{name}_mv", [P, NT, 2]),
                "var": self.sb(scope, f"{name}_var", [P, NT]), "rstd": self.sb(scope, f"{name}_rstd", [P, NT])}

    def transposed(self, x, hi, lo, banks, needs, free):
        marks = []
        for c in range(CK):
            ps = banks.take()
            self.pe.need(needs, ps.free)
            for t in range(NT):
                last = self.nc.tensor.transpose(ps.ap[:, t * P:(t + 1) * P], x[:, t, c * P:(c + 1) * P], self.ident)
            m = self.split_psum(ps.ap, hi[:, c, :], lo[:, c, :], self.pe.mark(last), free)
            release(ps, *m)
            marks += m
        return marks

    def load_split(self, scope, name, dram, chunks, width, stage, permute=False):
        hi = self.sb(scope, f"{name}_hi", [P, chunks, width], F32R)
        lo = self.sb(scope, f"{name}_lo", [P, chunks, width], F32R)
        st = stage.take()
        view = st.ap[:, 0:chunks * width]
        self.sp.need(st.free)
        m = self.stream(f"weights{st.index}").start(
            self.sp, view.rearrange("p (c n) -> p c n", c=chunks), dram.rearrange("(c p) n -> p c n", p=P))
        if not permute:
            v = view.rearrange("p (c n) -> p c n", c=chunks)
            m = self.split_sbuf(v, hi, lo, m)
        else:
            for c in range(chunks):
                src = st.ap[:, c * width:(c + 1) * width].rearrange("p (q h d) -> p q d h", h=4, d=DH)
                def dst(t):
                    return t[:, c, :].rearrange("p (q d h) -> p q d h", h=4, d=DH)
                m = self.split_sbuf(src, dst(hi), dst(lo), m)
        release(st, m)
        return {"hi": hi, "lo": lo, "ready": m}

    def load_bias_column(self, scope, name, dram):
        t = self.sb(scope, name, [P, CK])
        s = self.stream(name)
        v = dram.rearrange("(c q h d) -> c q d h", q=2, h=4, d=DH)
        for c in range(CK):
            for q in range(2):
                m = s.start(self.sp, t[64 * q:64 * q + 64, c:c + 1], v[c, q], allow_slow_non_contiguous=True)
        return t, m

    def load_row(self, scope, name, dram):
        t = self.sb(scope, name, [P, dram.shape[0]])
        m = self.stream(name).start(self.sp, t, dram.partition_broadcast(P))
        return t, m

    def context(self, scope, banks, pre):
        nc = self.nc
        hi = self.sb(scope, pre + "ctx_hi", [P, B, TC], F32R)
        lo = self.sb(scope, pre + "ctx_lo", [P, B, TC], F32R)
        with Temporary() as tmp:
            raw = self.sb(tmp, pre + "ctx_raw", [P, B // 2, CC])
            m = self.stream("ctx").start(self.sp, raw, self.inp["ctx_512"].rearrange("(a b) t c -> (b t) a c", b=2))
            per = min(B, 8)
            for g in range(B // per):
                ps = banks.take()
                self.pe.need(m, ps.free)
                for j in range(per // 2):
                    last = nc.tensor.transpose(ps.ap[:, j * P:(j + 1) * P], raw[:, per // 2 * g + j, :], self.ident)
                done = self.pe.mark(last)
                src = ps.ap[:, 0:per * TC].rearrange("p (b t) -> p b t", t=TC)
                marks = self.split_psum(src, hi[:, per * g:per * (g + 1), :], lo[:, per * g:per * (g + 1), :], done, None)
                release(ps, *marks)
            self.barrier()
        return {"hi": hi, "lo": lo}

    def context_keys(self, name, ctx, weight, bias, bias_ready, banks, scope):
        dram = self.nc.dram_tensor(f"{name}_keys", [2, C, B * TC], F32).ap()
        with Temporary() as tmp:
            stage = Ring(self.sbs(tmp, f"{name}_kstage", 2, [P, 2, min(B, 8) * TC], F32R))
            per = min(B, 8)
            for c in range(CK):
                for g in range(B // per):
                    ps = banks.take()
                    self.pe.need(weight["ready"], ps.free)
                    cols = slice(c * P, (c + 1) * P)
                    pairs = []
                    for a, b in (("hi", "hi"), ("lo", "hi"), ("hi", "lo")):
                        pairs.append((weight[a][:, 0, cols], ctx[b][:, per * g:per * (g + 1), :]))
                    done = self.pe.mark(self.product(ps.ap[:, 0:per * TC].rearrange("p (b t) -> p b t", t=TC), pairs))
                    st = stage.take()
                    m = self.split_psum(ps.ap[:, 0:per * TC], st.ap[:, 0, :], st.ap[:, 1, :], [done, bias_ready], st.free, bias=bias[:, c:c + 1])
                    release(ps, *m)
                    self.sp.need(m)
                    m = self.stream(f"kstage{st.index}").start(
                        self.sp, dram[:, c * P:(c + 1) * P, g * per * TC:(g + 1) * per * TC].rearrange("k r n -> r k n"), st.ap.bitcast(F32))
                    release(st, m)
            self.barrier()
        return dram

    def attention(self, layer):
        nc, pe, act, dve, pool, sp = self.nc, self.pe, self.act, self.dve, self.pool, self.sp
        own = layer == 0
        inp = self.inp
        pre = f"L{layer}_xattn_"
        with ExitStack() as scope:
            L = f"a{layer}_"
            score_banks = Ring([self.bank(0), self.bank(1)])
            prob_banks = Ring([self.bank(2, 2), self.bank(4, 2)])
            value_banks = Ring([self.bank(6)])
            banks = Ring([self.bank(7)])
            names = (dict(q="Wq", k="Wk", v="Wv", cq="Wcq", ck="Wck", cv="Wcv", o="Wp") if own
                     else dict(cq="Wq", ck="Wk", cv="Wv", o="Wo"))
            biases = {k: "b" + v[1:] for k, v in names.items()}
            W = {}
            with Temporary() as tmp:
                stage = Ring(self.sbs(tmp, L + "wstage", 2, [P, 2 * C]))
                for k in ("cq", "q", "k", "v", "cv", "o"):
                    if k in names:
                        chunks = 1 if k == "cv" else CK
                        W[k] = self.load_split(scope, L + "w" + k, inp[pre + names[k]], chunks, C, stage, permute=k in ("cq", "q", "k"))
                bias_col, bias_row = {}, {}
                for k in ("q", "k", "cq", "ck"):
                    if k in names:
                        bias_col[k] = self.load_bias_column(scope, L + "b" + k, inp[pre + biases[k]])
                for k in ("v", "cv", "o"):
                    if k in names:
                        bias_row[k] = self.load_row(scope, L + "b" + k, inp[pre + biases[k]])
                gate = self.gate[:, layer:layer + 1]
                ob, ready = bias_row["o"]
                dve.need(ready)
                dve.mark(nc.vector.tensor_scalar(ob, ob, gate, None, ALU.mult))
                ctx = self.context(tmp, banks, L)
                ctx_dram = nc.dram_tensor(L + "ctx_halves", [2, P, B * TC], F32).ap()
                for n, x in enumerate(("hi", "lo")):
                    self.stream("setup").start(sp, ctx_dram[n], ctx[x].rearrange("p b t -> p (b t)").bitcast(F32))
                wck = self.load_split(tmp, L + "wck", inp[pre + names["ck"]], 1, C, stage, permute=True)
                keys_dram = self.context_keys(f"ctx{layer}", ctx, wck, *bias_col["ck"], banks, tmp)
                self.barrier()

            nq = 8 if own else 4
            x_ring = Ring(self.sbs(scope, L + "x", 1, [P, NT, C]))
            residual = Ring(self.sbs(scope, L + "residual", 1, [P, NT, C]))
            xn = self.sb(scope, L + "xn", [P, NT, C])
            ctx_twice = self.sb(scope, L + "ctx_twice", [P, 2, 2, TC], F32R)
            stats = self.norm_scratch(scope, L + "ln")
            xT_hi = self.sb(scope, L + "xT_hi", [P, CK, T], F32R)
            xT_lo = self.sb(scope, L + "xT_lo", [P, CK, T], F32R)
            stage = Ring(self.sbs(scope, L + "stage", 3, [P, 2, T], F32R))
            Q = Ring(self.sbs(scope, L + "Q", 3, [KROWS, nq, T], F32R))
            if own:
                K = Ring(self.sbs(scope, L + "K", 3, [KROWS, 4, T], F32R))
                V = Ring(self.sbs(scope, L + "V", 2, [P, NT, H, VW]))
            KC = Ring(self.sbs(scope, L + "KC", 2, [KROWS, H, 2 * TC], F32R))
            VC = Ring(self.sbs(scope, L + "VC", 2, [P, H, VW]))
            probs = Ring(self.sbs(scope, L + "probs", 6, [P, 1024]))
            maxima = Ring(self.sbs(scope, L + "maxima", 2, [P, nq, NT]))
            minus_max = Ring(self.sbs(scope, L + "minus_max", 2, [nq * NT, 2, P], F32R))
            ysum = Ring(self.sbs(scope, L + "ysum", 1, [P, T]))
            recip = Ring(self.sbs(scope, L + "recip", 2, [P, 2, NT, 4]))
            ycross = self.sb(scope, L + "ycross", [P, NT, 4, DH])
            Y = Ring(self.sbs(scope, L + "Y", 2, [P, NT, C]))

            made = []
            if own:
                for s in K.slots:
                    made.append(dve.mark(nc.vector.memset(s.ap[ROWS:KROWS].bitcast(F32), 1.0)))
            for s in KC.slots:
                a = s.ap.bitcast(F32)
                made.append(dve.mark(nc.vector.memset(a, 0.0)))
                dve.need(made[-1])
                for r in range(2):
                    made.append(dve.mark(nc.vector.memset(a[ROWS:KROWS, r::2, r * TC:(r + 1) * TC], 1.0)))
            values = (list(V.slots) if own else []) + list(VC.slots)
            for s in values:
                m = pool.mark(nc.gpsimd.memset(s.ap, 0.0))
                pool.need(m)
                a = s.ap
                if s in VC.slots:
                    for r in range(2):
                        made.append(pool.mark(nc.gpsimd.memset(a[r * TC:(r + 1) * TC, r::2, DH:DH + 1], 1.0)))
                else:
                    made.append(pool.mark(nc.gpsimd.memset(a[:, :, :, DH:DH + 1], 1.0)))
            zero_rows = nc.dram_tensor(L + "zero_rows", [2, nq * T], F32).ap()
            m = pool.mark(nc.gpsimd.memset(xn, 0.0))
            sp.need(m)
            zero_src = xn.rearrange("p t c -> p (t c)")
            m = self.stream("setup").start(sp, zero_rows.rearrange("a (b n) -> (a b) n", n=1024), zero_src[0:2 * nq * T // 1024, :])
            for e in self.engines:
                e.need(made, m)
            scratch = {}
            for k in ("q", "cq", "k"):
                if k in names:
                    scratch[k] = nc.dram_tensor(f"{L}{k}_packed", [B, 2, C, T], F32).ap()
            x_in = inp["x"] if own else self.x2
            x_out = self.x1 if own else self.x3
            state = {b: {} for b in range(B)}
            unit = {u: {} for u in range(B * QUADS)}
            if not own:
                gathered = Ring(self.sbs(scope, L + "gathered", 2, [P, NT, C]))

            def prepare(b):
                st = state[b]
                xs = x_ring.take()
                sp.need(xs.free)
                m = self.stream(f"x{xs.index}").start(sp, xs.ap, x_in[b].rearrange("(t p) c -> p t c", p=P))
                if not own:
                    g = gathered.take()
                    pool.need(g.free)
                    s = self.stream(f"gather{g.index}")
                    for t in range(NT):
                        nc.gpsimd.indirect_dma_start(
                            out=g.ap[:, t, :], out_offset=None, in_=self.sorted_y[:],
                            in_offset=bass.IndirectOffsetOnAxis(ap=self.position[:, b * NT + t:b * NT + t + 1], axis=0)
                        ).then_inc(s.sem, 16)
                        s.count += 16
                    yield
                    dve.need(m, s.last())
                    m = dve.mark(nc.vector.scalar_tensor_tensor(
                        out=xs.ap, in0=g.ap, scalar=self.gate[:, 2:3], in1=xs.ap, op0=ALU.mult, op1=ALU.add))
                    release(g, m)
                yield
                m_norm = self.norm(xs.ap, xn, stats, m, state.get("xn_free"))
                pool.need(m_norm)
                m = pool.mark(nc.gpsimd.tensor_tensor(xs.ap, xs.ap, ob.unsqueeze(1).to_broadcast([P, NT, C]), ALU.add))
                sp.need(m)
                st["x_kept"] = self.stream("x_kept").start(sp, x_out[b].rearrange("(t p) c -> p t c", p=P), xs.ap)
                release(xs, st["x_kept"])
                yield
                xT = self.transposed(xn, xT_hi, xT_lo, banks, m_norm, state.get("xT_free"))
                state["xn_free"] = [(pe.sem, pe.count)]
                halves = {"hi": xT_hi, "lo": xT_lo}
                yield
                for k in ("q", "cq", "k"):
                    if k not in names:
                        continue
                    w, (bias, bias_ready) = W[k], bias_col[k]
                    for c in range(CK):
                        ps = banks.take()
                        pe.need(xT, w["ready"], ps.free)
                        pairs = [(w[a][:, kc, c * P:(c + 1) * P], halves[x][:, kc, :])
                                 for a, x in (("hi", "hi"), ("lo", "hi"), ("hi", "lo")) for kc in range(CK)]
                        done = pe.mark(self.product(ps.ap, pairs))
                        s = stage.take()
                        m = self.split_psum(ps.ap, s.ap[:, 0, :], s.ap[:, 1, :], [done, bias_ready], s.free, bias=bias[:, c:c + 1])
                        release(ps, *m)
                        sp.need(m)
                        m = self.stream(f"stage{s.index}").start(
                            sp, scratch[k][b, :, c * P:(c + 1) * P, :].rearrange("k r n -> r k n"), s.ap.bitcast(F32))
                        release(s, m)
                        st.setdefault("packed", []).append(m)
                        yield
                if own:
                    st["V"] = v = V.take()
                    bias, bias_ready = bias_row["v"]
                    for half in range(2):
                        ps = banks.take()
                        pe.need(xT, W["v"]["ready"], ps.free)
                        for j in range(2):
                            t = 2 * half + j
                            pairs = [(halves[x][:, kc, t * P:(t + 1) * P], W["v"][a][:, kc, :])
                                     for x, a in (("hi", "hi"), ("lo", "hi"), ("hi", "lo")) for kc in range(CK)]
                            last = self.product(ps.ap[:, j * C:(j + 1) * C], pairs)
                        dve.need(pe.mark(last), bias_ready, v.free)
                        m = dve.mark(nc.vector.tensor_tensor(
                            v.ap[:, 2 * half:2 * half + 2, :, 0:DH],
                            ps.ap.rearrange("p (t h d) -> p t h d", t=2, d=DH),
                            bias.rearrange("p (h d) -> p h d", d=DH).unsqueeze(1).to_broadcast([P, 2, H, DH]), ALU.add))
                        release(ps, m)
                        yield
                    st["V_ready"] = m
                state["xT_free"] = [(pe.sem, pe.count)]
                st["VC"] = v = VC.take()
                bias, bias_ready = bias_row["cv"]
                ps = banks.take()
                sp.need(state.get("twice_free"))
                for n in range(2):
                    m = self.stream("ctx_twice").start(sp, ctx_twice[:, n, :, :].bitcast(F32),
                                                       ctx_dram[n, :, b * TC:(b + 1) * TC].unsqueeze(1).to_broadcast([P, 2, TC]))
                pe.need(m, W["cv"]["ready"], ps.free)
                twice = {x: ctx_twice[:, n, :, :].rearrange("p r t -> p (r t)") for n, x in enumerate(("hi", "lo"))}
                pairs = [(twice[x], W["cv"][a][:, 0, :]) for x, a in (("hi", "hi"), ("lo", "hi"), ("hi", "lo"))]
                dve.need(pe.mark(self.product(ps.ap[:, 0:C], pairs)), bias_ready, v.free)
                state["twice_free"] = (pe.sem, pe.count)
                for r in range(2):
                    rows = slice(r * TC, (r + 1) * TC)
                    m = dve.mark(nc.vector.tensor_tensor(
                        v.ap[rows, r::2, 0:DH], ps.ap[rows, 0:C].rearrange("p (h d) -> p h d", d=DH)[:, r::2, :],
                        bias[rows].rearrange("p (h d) -> p h d", d=DH)[:, r::2, :], ALU.add))
                release(ps, m)
                st["VC_ready"] = m
                st["KC"] = kc = KC.take()
                sp.need(kc.free)
                s = self.stream(f"kc{kc.index}")
                for half in range(2):
                    src = keys_dram[half, :, b * TC:(b + 1) * TC].rearrange("(q d h) n -> d q h n", d=DH, h=4)
                    for rep in range(2):
                        r0 = (2 * half + rep) * DH
                        for odd in range(2):
                            for hh in range(2):
                                dst = kc.ap[r0:r0 + DH, 2 * hh + odd::4, odd * TC:(odd + 1) * TC].bitcast(F32)
                                m = s.start(sp, dst, src[:, :, 2 * hh + odd, :])
                st["KC_ready"] = m
                yield

            def pack(u):
                b, quad = divmod(u, QUADS)
                un, rows = unit[u], slice(64 * quad, 64 * quad + 64)
                un["Q"] = q = Q.take()
                sp.need(state[b]["packed"], q.free)
                s = self.stream(f"pack_q{q.index}")
                m = None
                for n, k in enumerate([k for k in ("q", "cq") if k in names]):
                    src = scratch[k][b, :, rows, :].rearrange("k (d h) n -> k d (h n)", h=4)
                    for rep in range(2):
                        m = s.start(sp, q.ap[rep * 2 * DH:(rep + 1) * 2 * DH, 4 * n:4 * n + 4, :].bitcast(F32), src)
                m = s.start(sp, q.ap[ROWS:KROWS, :, :].bitcast(F32), zero_rows)
                un["ready"] = [m]
                if own:
                    un["K"] = k_ = K.take()
                    sp.need(k_.free)
                    src = scratch["k"][b, :, rows, :].rearrange("k (d h) n -> k d (h n)", h=4)
                    for half in range(2):
                        m = self.stream(f"pack_k{k_.index}").start(
                            sp, k_.ap[half * 2 * DH:(half + 1) * 2 * DH].bitcast(F32),
                            src[half].unsqueeze(0).to_broadcast([2, DH, 4 * T]))
                    un["ready"].append(m)
                yield

            def find_max(u):
                b, quad = divmod(u, QUADS)
                un, st = unit[u], state[b]
                q = un["Q"].ap
                kc = st["KC"].ap
                mx = maxima.take()
                dve.need(mx.free)
                tasks = []
                if own:
                    tasks += [(3, [h]) for h in range(4)] + [(2, [h]) for h in range(4)]
                    tasks += [(1, [0, 1]), (1, [2, 3]), (0, [0, 1, 2, 3])]
                c0 = 4 if own else 0
                for i, heads in tasks:
                    n = (i + 1) * P
                    ps = score_banks.take()
                    pe.need(un["ready"], ps.free)
                    for j, h in enumerate(heads):
                        out = ps.ap[:, j * n:(j + 1) * n]
                        nc.tensor.matmul(out, q[:, h, i * P:(i + 1) * P], un["K"].ap[:, h, 0:n], start=True, stop=False)
                        last = nc.tensor.matmul(out[:, i * P:n], self.ident16, self.mask_qk, start=False, stop=True)
                    dve.need(pe.mark(last))
                    m = dve.mark(nc.vector.tensor_reduce(
                        mx.ap[:, heads[0]:heads[-1] + 1, i:i + 1].rearrange("p h i -> p (h i)"),
                        ps.ap[:, 0:len(heads) * n].rearrange("p (h n) -> p h n", n=n), AXIS, ALU.max))
                    release(ps, m)
                    yield
                for i in (0, 2):
                    ps = score_banks.take()
                    pe.need(un["ready"], st["KC_ready"], ps.free)
                    for j in range(2):
                        for h in range(4):
                            odd = h % 2
                            last = nc.tensor.matmul(
                                ps.ap[:, (h * 2 + j) * TC:(h * 2 + j + 1) * TC], q[:, c0 + h, (i + j) * P:(i + j + 1) * P],
                                kc[:, 4 * quad + h, odd * TC:(odd + 1) * TC], start=True, stop=True)
                    dve.need(pe.mark(last))
                    m = dve.mark(nc.vector.tensor_reduce(
                        mx.ap[:, c0:c0 + 4, i:i + 2], ps.ap.rearrange("p (h j n) -> p h j n", h=4, j=2), AXIS, ALU.max))
                    release(ps, m)
                    yield
                ps = banks.take()
                pe.need(m, ps.free)
                n = nq * NT
                done = pe.mark(nc.tensor.transpose(ps.ap[0:n, 0:P], mx.ap.rearrange("p h i -> p (h i)"), self.ident))
                release(mx, done)
                mm = minus_max.take()
                act.need(done, mm.free)
                m_hi = act.mark(nc.scalar.activation(mm.ap[:, 0, :], ps.ap[0:n, 0:P], ACT.Copy, scale=-1.0))
                dve.need(m_hi)
                m_lo = dve.mark(nc.vector.scalar_tensor_tensor(
                    out=mm.ap[:, 1, :], in0=ps.ap[0:n, 0:P], scalar=-1.0, in1=mm.ap[:, 0, :].bitcast(F32),
                    op0=ALU.mult, op1=ALU.subtract))
                release(ps, m_lo)
                sp.need(m_lo, (pe.sem, pe.count))
                s = self.stream(f"max{mm.index}")
                for half in range(2):
                    m = s.start(sp, q[ROWS + half:ROWS + half + 1].rearrange("p h (i n) -> p (h i) n", n=P).bitcast(F32),
                                mm.ap[:, half, :].bitcast(F32))
                release(mm, m)
                un["max_ready"] = m
                yield

            def attend(u):
                b, quad = divmod(u, QUADS)
                un, st = unit[u], state[b]
                q = un["Q"].ap
                kc, vc = st["KC"].ap, st["VC"].ap
                c0 = 4 if own else 0
                if quad == 0:
                    st["Y"] = Y.take()
                y = st["Y"]
                r = recip.take()

                def exponent(ps, n_el, done, view=None):
                    pr = probs.take()
                    act.need(done, pr.free)
                    src, dst = ps.ap, pr.ap
                    if view is not None:
                        src, dst = view(src), view(dst)
                    else:
                        src, dst = src[:, 0:n_el], dst[:, 0:n_el]
                    m = act.mark(nc.scalar.activation(dst, src, ACT.Exp, scale=SCALE))
                    release(ps, m)
                    return pr, m

                def quotient(acc, done, which):
                    ys = ysum.take()
                    act.need(done, ys.free)
                    m = act.mark(nc.scalar.activation(ys.ap, acc.ap, ACT.Copy))
                    release(acc, m)
                    ps = banks.take()
                    pe.need(m, ps.free)
                    for i in range(NT):
                        last = nc.tensor.transpose(ps.ap[:, i * P:(i + 1) * P], ys.ap[:, i * P:(i + 1) * P], self.ident)
                    done = pe.mark(last)
                    release(ys, done)
                    v = ps.ap.rearrange("p (i h w) -> p i h w", i=NT, w=VW)
                    dve.need(done, r.free)
                    m = dve.mark(nc.vector.reciprocal(r.ap[:, which], v[:, :, :, DH]))
                    dve.need(m)
                    inv = r.ap[:, which].unsqueeze(3).to_broadcast([P, NT, 4, DH])
                    out = y.ap[:, :, 64 * quad:64 * quad + 64].rearrange("p i (h d) -> p i h d", d=DH)
                    if which == 0:
                        dve.need(y.free)
                        m = dve.mark(nc.vector.tensor_tensor(out, v[:, :, :, 0:DH], inv, ALU.mult))
                    else:
                        m = dve.mark(nc.vector.tensor_tensor(ycross, v[:, :, :, 0:DH], inv, ALU.mult))
                        dve.need(m)
                        m = dve.mark(nc.vector.tensor_tensor(out, out, ycross, ALU.add))
                    release(ps, m)
                    return m

                if own:
                    v_ = st["V"].ap
                    acc = value_banks.take()
                    for kt in range(NT):
                        n = T - kt * P
                        per = {0: 2, 1: 2, 2: 4, 3: 4}[kt]
                        width = {0: 512, 1: 512, 2: 256, 3: 128}[kt]
                        pieces = []
                        for h0 in range(0, 4, per):
                            ps = prob_banks.take()
                            pe.need(un["max_ready"], un["ready"], ps.free)
                            for j in range(per):
                                h = h0 + j
                                out = ps.ap[:, j * width:j * width + n]
                                nc.tensor.matmul(out, un["K"].ap[:, h, kt * P:(kt + 1) * P], q[:, h, kt * P:T], start=True, stop=False)
                                last = nc.tensor.matmul(out[:, 0:P], self.ident16, self.mask_kq, start=False, stop=True)
                            done = pe.mark(last)
                            view = (lambda a, n=n: a.rearrange("p (j w) -> p j w", w=512)[:, :, 0:n]) if kt < 2 else None
                            pieces.append(exponent(ps, per * n, done, view))
                            yield
                        pe.need(st["V_ready"], *[m for _, m in pieces])
                        if kt == 0:
                            pe.need(acc.free)
                        for j, (pr, _) in enumerate(pieces):
                            for jj in range(per):
                                h = j * per + jj
                                last = nc.tensor.matmul(
                                    acc.ap[VW * h:VW * h + VW, kt * P:T], v_[:, kt, 4 * quad + h, :],
                                    pr.ap[:, jj * width:jj * width + n], start=kt == 0, stop=kt == NT - 1)
                        done = pe.mark(last)
                        for pr, _ in pieces:
                            release(pr, done)
                        yield
                    release(un["K"], done)
                    quotient(acc, done, 0)
                    yield
                ps = prob_banks.take()
                pe.need(un["max_ready"], un["ready"], ps.free)
                for pair in range(2):
                    out = ps.ap[:, pair * T:(pair + 1) * T]
                    for odd in range(2):
                        h = 2 * pair + odd
                        last = nc.tensor.matmul(out, kc[:, 4 * quad + h, :], q[:, c0 + h, :], start=odd == 0, stop=odd == 1)
                done = pe.mark(last)
                release(un["Q"], done)
                pr, m = exponent(ps, 2 * T, done)
                yield
                acc = value_banks.take()
                pe.need(m, st["VC_ready"], acc.free)
                for h in range(4):
                    last = nc.tensor.matmul(acc.ap[VW * h:VW * h + VW, :], vc[:, 4 * quad + h, :],
                                            pr.ap[:, (h // 2) * T:(h // 2 + 1) * T], start=True, stop=True)
                done = pe.mark(last)
                release(pr, done)
                m = quotient(acc, done, 1 if own else 0)
                release(r, m)
                st["Y_ready"] = m
                if quad == QUADS - 1:
                    release(st["KC"], done)
                    release(st["VC"], done)
                    if own:
                        release(st["V"], done)
                yield

            def finish(b):
                st = state[b]
                y = st["Y"]
                xs = residual.take()
                sp.need(st["x_kept"], xs.free)
                x_ready = self.stream("residual").start(sp, xs.ap, x_out[b].rearrange("(t p) c -> p t c", p=P))
                hi, lo = stage.take(), stage.take()
                yT = self.transposed(y.ap, hi.ap, lo.ap, banks, st["Y_ready"], [hi.free, lo.free])
                release(y, (pe.sem, pe.count))
                halves = {"hi": hi.ap, "lo": lo.ap}
                for half in range(2):
                    ps = banks.take()
                    pe.need(yT, W["o"]["ready"], ps.free)
                    for j in range(2):
                        t = 2 * half + j
                        pairs = [(halves[x][:, kc, t * P:(t + 1) * P], W["o"][a][:, kc, :])
                                 for x, a in (("hi", "hi"), ("lo", "hi"), ("hi", "lo")) for kc in range(CK)]
                        last = self.product(ps.ap[:, j * C:(j + 1) * C], pairs)
                    done = pe.mark(last)
                    dve.need(done, x_ready)
                    two = xs.ap[:, 2 * half:2 * half + 2, :]
                    m = dve.mark(nc.vector.scalar_tensor_tensor(
                        out=two, in0=ps.ap.rearrange("p (t c) -> p t c", t=2), scalar=gate, in1=two, op0=ALU.mult, op1=ALU.add))
                    release(ps, m)
                release(hi, done)
                release(lo, done)
                yield
                sp.need(m)
                m = self.stream(f"x_out{xs.index}").start(sp, x_out[b].rearrange("(t p) c -> p t c", p=P), xs.ap)
                release(xs, m)
                yield

            plan = Plan()
            for b in range(B):
                plan.add(QUADS * b - 4.6, 3.8, 13 if own else 6, prepare(b))
                plan.add(QUADS * b + QUADS + 1.8, 1.0, 2, finish(b))
            for u in range(B * QUADS):
                plan.add(u - 0.6, 0.1, 1, pack(u))
                plan.add(u, 1.0, 14 if own else 3, find_max(u))
                plan.add(u + 1.5, 1.0, 13 if own else 2, attend(u))
            plan.run()
            self.barrier()

    def route_and_share(self, scope):
        nc, pe, act, dve, pool, sp = self.nc, self.pe, self.act, self.dve, self.pool, self.sp
        inp = self.inp
        banks = Ring([self.bank(i) for i in range(2)])
        wide = Ring([self.bank(i) for i in range(2, 8)])
        self.position = self.sb(scope, "position", [P, NTILES], I32)
        self.slot_expert = self.sb(scope, "slot_expert", [1, SLOTS], I32)
        with ExitStack() as mine:
            stage = Ring(self.sbs(mine, "m_wstage", 2, [P, 2 * HID]))
            GW = self.load_split(mine, "m_router", inp["L0_ffn_gate_w"], CK, E, stage)
            SG = self.load_split(mine, "m_sgate", inp["L0_ffn_shared_gate_w"], CK, HID, stage)
            SU = self.load_split(mine, "m_sup", inp["L0_ffn_shared_up_w"], CK, HID, stage)
            SD = self.load_split(mine, "m_sdown", inp["L0_ffn_shared_down_w"], HK, C, stage)
            scaled = self.sb(mine, "m_scaled", [P, NTILES, C])
            onehot = self.sb(mine, "m_onehot", [P, NTILES, E])
            prefix = self.sb(mine, "m_prefix", [P, NTILES + 1, E], BF16)
            rank = self.sb(mine, "m_rank", [P, NTILES])
            x_ring = Ring(self.sbs(mine, "m_x", 2, [P, NT, C]))
            xn = self.sb(mine, "m_xn", [P, NT, C])
            stats = self.norm_scratch(mine, "m_ln")
            xT = [Ring(self.sbs(mine, f"m_xT{n}", 2, [P, CK, T], F32R)) for n in ("hi", "lo")]
            hT = [Ring(self.sbs(mine, f"m_hT{n}", 2, [P, HK, T], F32R)) for n in ("hi", "lo")]
            act_out = Ring(self.sbs(mine, "m_silu", 2, [P, T]))
            hidden = Ring(self.sbs(mine, "m_hidden", 2, [P, T]))
            descending = self.sb(mine, "m_descending", [P, E])
            small = {n: self.sb(mine, "m_" + n, [P, NT, E]) for n in ("equal", "first", "work")}
            smallv = {n: self.sb(mine, "m_" + n, [P, NT]) for n in ("top", "best", "score")}
            onehot16 = self.sb(mine, "m_onehot16", [P, NT, E], BF16)
            asc = self.sb(mine, "m_asc", [P, E], I32)
            m = pool.mark(nc.gpsimd.iota(asc, pattern=[[-1, E]], base=E, channel_multiplier=0))
            dve.need(m)
            m1 = dve.mark(nc.vector.tensor_copy(descending, asc))
            m2 = dve.mark(nc.vector.memset(prefix[:, 0, :], 0.0))
            m3 = dve.mark(nc.vector.memset(xn, 0.0))
            dve.need(m1, m2, m3)
            sp.need(m3)
            zero = xn.rearrange("p t c -> p (t c)")
            rows = self.sorted_x.rearrange("(s p) c -> p s c", p=P)
            zeroed = None
            for s0 in range(0, SLOTS, NT):
                n = min(NT, SLOTS - s0)
                zeroed = self.stream("zero_sorted").start(sp, rows[:, s0:s0 + n, :], xn[:, 0:n, :])
            dve.need(zeroed)
            self.zeroed = zeroed
            loaded = {}

            def load(g):
                x = x_ring.take()
                sp.need(x.free)
                loaded[g] = (x, self.stream(f"m_x{x.index}").start(sp, x.ap, self.x1[g].rearrange("(t p) c -> p t c", p=P)))

            keep = {}

            def router(g):
                x, m_x = loaded[g]
                m_norm = self.norm(x.ap, xn, stats, m_x, keep.get("xn_free"))
                hi, lo = xT[0].take(), xT[1].take()
                ready = self.transposed(xn, hi.ap, lo.ap, banks, m_norm, [hi.free, lo.free])
                xh = {"hi": hi.ap, "lo": lo.ap}
                ps = banks.take()
                pe.need(ready, GW["ready"], ps.free)
                for t in range(NT):
                    pairs = [(xh[a][:, kc, t * P:(t + 1) * P], GW[w][:, kc, :])
                             for a, w in (("hi", "hi"), ("lo", "hi"), ("hi", "lo")) for kc in range(CK)]
                    last = self.product(ps.ap[:, t * E:(t + 1) * E], pairs)
                logits = ps.ap[:, 0:NT * E].rearrange("p (t e) -> p t e", e=E)
                top, best, score = smallv["top"], smallv["best"], smallv["score"]
                eq, first, work = small["equal"], small["first"], small["work"]

                def wide_(v):
                    return v.unsqueeze(2).to_broadcast([P, NT, E])
                dve.need(pe.mark(last), keep.get("score_read"))
                m = dve.mark(nc.vector.tensor_reduce(top, logits, AXIS, ALU.max))
                act.need(m, keep.get("scaled"))
                m_score = act.mark(nc.scalar.activation(score, top, ACT.Sigmoid))
                dve.need(m)
                m = dve.mark(nc.vector.tensor_tensor(eq, logits, wide_(top), ALU.is_equal))
                release(ps, m)
                dve.need(m)
                m = dve.mark(nc.vector.tensor_tensor(first, eq, descending.unsqueeze(1).to_broadcast([P, NT, E]), ALU.mult))
                dve.need(m)
                m = dve.mark(nc.vector.tensor_reduce(best, first, AXIS, ALU.max))
                dve.need(m)
                tiles = slice(g * NT, (g + 1) * NT)
                m = dve.mark(nc.vector.tensor_tensor(onehot[:, tiles, :], first, wide_(best), ALU.is_equal))
                dve.need(m, keep.get("ranked"))
                m_hot = dve.mark(nc.vector.tensor_copy(onehot16, onehot[:, tiles, :]))
                for t in range(NT):
                    n = g * NT + t
                    m = dve.mark(nc.vector.tensor_tensor(prefix[:, n + 1, :], prefix[:, n, :], onehot[:, n, :], ALU.add))
                    dve.need(m)
                ps = banks.take()
                pe.need(m_hot, m, ps.free)
                for t in range(NT):
                    out = ps.ap[:, t * E:(t + 1) * E]
                    nc.tensor.matmul(out, self.before, onehot16[:, t, :], start=True, stop=False)
                    last = nc.tensor.matmul(out, self.ones16, prefix[:, g * NT + t, :], start=False, stop=True)
                keep["ranked"] = done = pe.mark(last)
                dve.need(done)
                m = dve.mark(nc.vector.tensor_tensor(work, ps.ap[:, 0:NT * E].rearrange("p (t e) -> p t e", e=E), onehot[:, tiles, :], ALU.mult))
                release(ps, m)
                dve.need(m)
                m = dve.mark(nc.vector.tensor_reduce(rank[:, tiles], work, AXIS, ALU.add))
                act.need(m_score)
                for t in range(NT):
                    m = act.mark(nc.scalar.activation(scaled[:, g * NT + t, :], xn[:, t, :], ACT.Copy, scale=score[:, t:t + 1]))
                keep["scaled"] = m
                keep["score_read"] = m_score
                keep["xn_free"] = [m, (pe.sem, pe.count)]
                return hi, lo, ready

            def shared(g, hi, lo, ready):
                x, m_x = loaded[g]
                xh = {"hi": hi.ap, "lo": lo.ap}
                hh, hl = hT[0].take(), hT[1].take()
                marks = []
                for mchunk in range(HK):
                    cols = slice(mchunk * P, (mchunk + 1) * P)
                    outs = []
                    for W in (SG, SU):
                        ps = wide.take()
                        pe.need(ready, W["ready"], ps.free)
                        pairs = [(W[w][:, kc, cols], xh[a][:, kc, :])
                                 for w, a in (("hi", "hi"), ("lo", "hi"), ("hi", "lo")) for kc in range(CK)]
                        outs.append((ps, pe.mark(self.product(ps.ap, pairs))))
                    so, hd = act_out.take(), hidden.take()
                    (pg, mg), (pu, mu) = outs
                    act.need(mg, so.free)
                    m = act.mark(nc.scalar.activation(so.ap, pg.ap, ACT.Silu))
                    release(pg, m)
                    dve.need(m, mu, hd.free)
                    m = dve.mark(nc.vector.tensor_tensor(hd.ap, pu.ap, so.ap, ALU.mult))
                    release(pu, m)
                    release(so, m)
                    act.need(m, hh.free)
                    m1 = act.mark(nc.scalar.activation(hh.ap[:, mchunk, :], hd.ap, ACT.Copy))
                    dve.need(m1, hl.free)
                    m2 = dve.mark(nc.vector.tensor_tensor(hl.ap[:, mchunk, :], hd.ap, hh.ap[:, mchunk, :].bitcast(F32), ALU.subtract))
                    release(hd, m2)
                    marks += [m1, m2]
                release(hi, (pe.sem, pe.count))
                release(lo, (pe.sem, pe.count))
                hs = {"hi": hh.ap, "lo": hl.ap}
                for half in range(2):
                    ps = wide.take()
                    pe.need(marks, SD["ready"], ps.free)
                    for j in range(2):
                        t = 2 * half + j
                        pairs = [(hs[a][:, kc, t * P:(t + 1) * P], SD[w][:, kc, :])
                                 for a, w in (("hi", "hi"), ("lo", "hi"), ("hi", "lo")) for kc in range(HK)]
                        last = self.product(ps.ap[:, j * C:(j + 1) * C], pairs)
                    done = pe.mark(last)
                    dve.need(done)
                    two = x.ap[:, 2 * half:2 * half + 2, :]
                    m = dve.mark(nc.vector.scalar_tensor_tensor(
                        out=two, in0=ps.ap.rearrange("p (t c) -> p t c", t=2), scalar=self.gate[:, 2:3], in1=two,
                        op0=ALU.mult, op1=ALU.add))
                    release(ps, m)
                release(hh, done)
                release(hl, done)
                sp.need(m)
                m = self.stream(f"m_xo{x.index}").start(sp, self.x2[g].rearrange("(t p) c -> p t c", p=P), x.ap)
                release(x, m)

            load(0)
            load(1)
            nxt = router(0)
            for g in range(B):
                cur = nxt
                if g + 1 < B:
                    nxt = router(g + 1)
                shared(g, *cur)
                if g + 2 < B:
                    load(g + 2)
            ps = banks.take()
            pe.need((dve.sem, dve.count), ps.free)
            done = pe.mark(nc.tensor.matmul(ps.ap[:, 0:E], self.ones16, prefix[:, NTILES, :], start=True, stop=True))
            ends = self.sbs(mine, "m_ends", 2, [P, E])
            counts = self.sbs(mine, "m_counts", 2, [P, E], I32)
            slots = self.sb(mine, "m_slots", [P, E])
            first = self.sb(mine, "m_first_row", [P, E])

            def step(instruction):
                m = dve.mark(instruction)
                dve.need(m)
                return m
            dve.need(done)
            step(nc.vector.tensor_scalar(counts[0], ps.ap[:, 0:E], float(P - 1), None, ALU.add))
            step(nc.vector.tensor_scalar(counts[1], counts[0], 7, None, ALU.logical_shift_right))
            step(nc.vector.tensor_copy(slots, counts[1]))
            step(nc.vector.tensor_copy(ends[0], slots))
            cur, shift = 0, 1
            while shift < E:
                a, b = ends[cur], ends[1 - cur]
                step(nc.vector.tensor_copy(b[:, 0:shift], a[:, 0:shift]))
                step(nc.vector.tensor_tensor(b[:, shift:E], a[:, shift:E], a[:, 0:E - shift], ALU.add))
                cur, shift = 1 - cur, 2 * shift
            end = ends[cur]
            step(nc.vector.tensor_tensor(first, end, slots, ALU.subtract))
            step(nc.vector.tensor_scalar(first, first, float(P), None, ALU.mult))
            step(nc.vector.tensor_tensor(onehot, onehot, first.unsqueeze(1).to_broadcast([P, NTILES, E]), ALU.mult))
            base = self.sb(mine, "m_base", [P, NTILES])
            step(nc.vector.tensor_reduce(base, onehot, AXIS, ALU.add))
            step(nc.vector.tensor_tensor(base, base, rank, ALU.add))
            m_pos = step(nc.vector.tensor_copy(self.position, base))
            sl_i = self.sb(mine, "m_sloti", [1, SLOTS], I32)
            sl_f = self.sb(mine, "m_slotf", [1, SLOTS])
            cmp = self.sb(mine, "m_cmp", [1, SLOTS, E])
            cnt = self.sb(mine, "m_cnt", [1, SLOTS])
            dve.need(pool.mark(nc.gpsimd.iota(sl_i, pattern=[[1, SLOTS]], base=0, channel_multiplier=0)))
            step(nc.vector.tensor_copy(sl_f, sl_i))
            step(nc.vector.tensor_tensor(cmp, end[0:1].unsqueeze(1).to_broadcast([1, SLOTS, E]),
                                         sl_f.unsqueeze(2).to_broadcast([1, SLOTS, E]), ALU.is_le))
            step(nc.vector.tensor_reduce(cnt, cmp, AXIS, ALU.add))
            step(nc.vector.tensor_scalar(cnt, cnt, float(E - 1), None, ALU.min))
            step(nc.vector.tensor_copy(self.slot_expert, cnt))
            pool.need(m_pos, (act.sem, act.count), self.zeroed)
            s = self.stream("scatter")
            for t in range(NTILES):
                nc.gpsimd.indirect_dma_start(
                    out=self.sorted_x[:], out_offset=bass.IndirectOffsetOnAxis(ap=self.position[:, t:t + 1], axis=0),
                    in_=scaled[:, t, :], in_offset=None).then_inc(s.sem, 16)
                s.count += 16
            self.barrier()

    def experts(self):
        nc, pe, act, dve, pool, sp = self.nc, self.pe, self.act, self.dve, self.pool, self.sp
        inp = self.inp
        with ExitStack() as scope:
            wg = Ring(self.sbs(scope, "e_gate", 3, [P, CK, HID]))
            wu = Ring(self.sbs(scope, "e_up", 3, [P, CK, HID]))
            wd = Ring(self.sbs(scope, "e_down", 3, [P, HK, C]))
            xr = Ring(self.sbs(scope, "e_x", 3, [P, C]))
            xT = Ring(self.sbs(scope, "e_xT", 2, [P, CK, P]))
            so = Ring(self.sbs(scope, "e_silu", 2, [P, HID]))
            hd = Ring(self.sbs(scope, "e_hidden", 2, [P, HID]))
            hT = Ring(self.sbs(scope, "e_hT", 2, [P, HK, P]))
            yo = Ring(self.sbs(scope, "e_y", 2, [P, C]))
            turn = Ring([self.bank(0), self.bank(1)])
            up = Ring([self.bank(i) for i in (2, 3, 4, 5)])
            down = Ring([self.bank(6), self.bank(7)])
            loads = {}

            def load(j):
                a, b, c, x = wg.take(), wu.take(), wd.take(), xr.take()
                e = sp.q.value_load(self.slot_expert[0:1, j:j + 1], min_val=0, max_val=E - 1)
                marks = []
                for slot, name, tag in ((a, "routed_gate_w", "g"), (b, "routed_up_w", "u"), (c, "routed_down_w", "d")):
                    sp.need(slot.free)
                    marks.append(self.stream(f"e_{tag}{slot.index}").start(
                        sp, slot.ap, inp["L0_ffn_" + name][bass.DynSlice(e, 1)].rearrange("e (c p) n -> p (e c) n", p=P)))
                sp.need(x.free)
                marks.append(self.stream(f"e_x{x.index}").start(sp, x.ap, self.sorted_x[j * P:(j + 1) * P, :]))
                loads[j] = (a, b, c, x, marks)

            st = {}

            def first(j):
                a, b, c, x, (mg, mu, md, mx) = loads[j]
                ps = turn.take()
                pe.need(mx, ps.free)
                for k in range(CK):
                    last = nc.tensor.transpose(ps.ap[:, k * P:(k + 1) * P], x.ap[:, k * P:(k + 1) * P], self.ident)
                done = pe.mark(last)
                release(x, done)
                t = xT.take()
                act.need(done, t.free)
                m = act.mark(nc.scalar.activation(t.ap, ps.ap[:, 0:C].rearrange("p (c n) -> p c n", c=CK), ACT.Copy))
                release(ps, m)
                st[j] = dict(xT=t, ready=m)

            def second(j):
                a, b, c, x, (mg, mu, md, mx) = loads[j]
                t, m = st[j]["xT"], st[j]["ready"]
                pg, pu = up.take(), up.take()
                pe.need(m, mg, pg.free)
                g = pe.mark(self.product(pg.ap, [(t.ap[:, k, :], a.ap[:, k, :]) for k in range(CK)]))
                pe.need(mu, pu.free)
                u = pe.mark(self.product(pu.ap, [(t.ap[:, k, :], b.ap[:, k, :]) for k in range(CK)]))
                release(a, g)
                release(b, u)
                release(t, u)
                s, h = so.take(), hd.take()
                act.need(g, s.free)
                m = act.mark(nc.scalar.activation(s.ap, pg.ap, ACT.Silu))
                release(pg, m)
                dve.need(m, u, h.free)
                m = dve.mark(nc.vector.tensor_tensor(h.ap, pu.ap, s.ap, ALU.mult))
                release(pu, m)
                release(s, m)
                st[j].update(h=h, h_ready=m)

            def third(j):
                a, b, c, x, (mg, mu, md, mx) = loads[j]
                h = st[j]["h"]
                ps = turn.take()
                pe.need(st[j]["h_ready"], ps.free)
                for k in range(HK):
                    last = nc.tensor.transpose(ps.ap[:, k * P:(k + 1) * P], h.ap[:, k * P:(k + 1) * P], self.ident)
                done = pe.mark(last)
                release(h, done)
                t = hT.take()
                dve.need(done, t.free)
                m = dve.mark(nc.vector.tensor_copy(t.ap, ps.ap.rearrange("p (c n) -> p c n", c=HK)))
                release(ps, m)
                st[j].update(hT=t, hT_ready=m)

            def fourth(j):
                a, b, c, x, (mg, mu, md, mx) = loads[j]
                t = st[j]["hT"]
                ps = down.take()
                pe.need(st[j]["hT_ready"], md, ps.free)
                done = pe.mark(self.product(ps.ap[:, 0:C], [(t.ap[:, k, :], c.ap[:, k, :]) for k in range(HK)]))
                release(c, done)
                release(t, done)
                y = yo.take()
                act.need(done, y.free)
                m = act.mark(nc.scalar.activation(y.ap, ps.ap[:, 0:C], ACT.Copy))
                release(ps, m)
                act.need(m)
                m = self.stream(f"e_y{y.index}").start(act, self.sorted_y[j * P:(j + 1) * P, :], y.ap)
                release(y, m)

            for j in range(-1, SLOTS + 3):
                if j == -1:
                    load(0)
                    load(1)
                    first(0)
                if 0 <= j < SLOTS:
                    second(j)
                if 0 <= j - 1 < SLOTS:
                    third(j - 1)
                if 0 <= j + 1 < SLOTS and j >= 0:
                    first(j + 1)
                if 0 <= j - 1 < SLOTS:
                    fourth(j - 1)
                if 0 <= j and j + 2 < SLOTS:
                    load(j + 2)
            self.barrier()

    def feed_forward(self):
        nc, pe, act, dve, pool, sp = self.nc, self.pe, self.act, self.dve, self.pool, self.sp
        inp = self.inp
        with ExitStack() as scope:
            banks = Ring([self.bank(i) for i in range(8)])
            shapes = dict(w1=(DH1, C), w2=(DH1, C), h1=(DH1, DH1), h2=(DH1, DH1), w3=(C, DH1))
            W, lo_dram, S = {}, {}, {}
            odd = self.sb(scope, "f_odd", [P, 64])
            zeroed = dve.mark(nc.vector.memset(odd, 0.0))
            column = 0
            with Temporary() as tmp:
                rows = Ring(self.sbs(tmp, "f_rows", 3, [P, 4, 512]))
                los = Ring(self.sbs(tmp, "f_los", 3, [P, 512]))
                scr = self.sb(tmp, "f_scr", [P, 512])
                for name, (o, i) in shapes.items():
                    W[name] = hi = self.sb(scope, f"f_{name}", [P, i // P, o], F32R)
                    lo_dram[name] = nc.dram_tensor(f"f_{name}_lo", [P, i // P, o], F32).ap()
                    per_i = min(i, 512)
                    per_o = min(o, 512)
                    for o0 in range(0, o, per_o):
                        for i0 in range(0, i, per_i):
                            nb = per_o // P
                            r = rows.take()
                            sp.need(r.free)
                            m = self.stream(f"f_rows{r.index}").start(
                                sp, r.ap[:, 0:nb, 0:per_i], inp[f"L1_ffn_{name}_w"][o0:o0 + per_o, i0:i0 + per_i].rearrange("(t p) i -> p t i", p=P))
                            for c in range(per_i // P):
                                ps = banks.take()
                                pe.need(m, ps.free)
                                for t in range(nb):
                                    last = nc.tensor.transpose(ps.ap[:, t * P:(t + 1) * P], r.ap[:, t, c * P:(c + 1) * P], self.ident)
                                done = pe.mark(last)
                                src = ps.ap[:, 0:per_o]
                                dst = hi[:, i0 // P + c, o0:o0 + per_o]
                                l = los.take()
                                lo = l.ap[:, 0:per_o]
                                ms = self.split_psum(src, dst, lo, done, l.free)
                                release(ps, *ms)
                                dve.need(ms, zeroed)
                                mm = dve.mark(nc.vector.tensor_scalar(scr[:, 0:per_o], lo, 0.0, None, ALU.not_equal, ALU.add,
                                                                      accum_out=odd[:, column:column + 1]))
                                column += 1
                                sp.need(ms)
                                md = self.stream(f"f_lo{l.index}").start(sp, lo_dram[name][:, i0 // P + c, o0:o0 + per_o], lo)
                                release(l, mm, md)
                            release(r, done)
                self.barrier()
            ps = banks.take()
            pe.need(ps.free)
            total = self.sb(scope, "f_total", [P, 1])
            flag = self.sb(scope, "f_flag", [1, 1], I32)
            m = dve.mark(nc.vector.tensor_reduce(total, odd, AXIS, ALU.add))
            pe.need(m)
            done = pe.mark(nc.tensor.matmul(ps.ap[0:1, 0:1], total, self.ones[:, 0:1], start=True, stop=True))
            dve.need(done)
            m = dve.mark(nc.vector.tensor_scalar(flag, ps.ap[0:1, 0:1], 1.0, None, ALU.min))
            release(ps, m)
            pe.need(m)
            sp.need(m)
            wider = nc.values_load(flag[0:1, 0:1], engines=[mybir.EngineType.SP, mybir.EngineType.PE], min_val=0, max_val=1)

            for name in ("w1", "w2", "h1", "h2"):
                S[name] = self.sb(scope, f"f_s_{name}", [P, DK])
                m = self.stream("f_scales").start(sp, S[name], inp[f"L1_ffn_{name}_s"].rearrange("(c p) -> p c", p=P), allow_slow_non_contiguous=True)
            s3, m3 = self.load_row(scope, "f_s3", inp["L1_ffn_w3_s"])
            dve.need(m3)
            m3 = dve.mark(nc.vector.tensor_scalar(s3, s3, self.gate[:, 3:4], None, ALU.mult))
            for e in self.engines:
                e.need(m, m3)

            x_ring = Ring(self.sbs(scope, "f_x", 2, [P, NT, C]))
            xn = self.sb(scope, "f_xn", [P, NT, C])
            stats = self.norm_scratch(scope, "f_ln")
            xT = [Ring(self.sbs(scope, f"f_xT{n}", 1, [P, CK, T], F32R)) for n in ("hi", "lo")]
            hs = [Ring(self.sbs(scope, f"f_h{n}", 2, [P, DK, T], F32R)) for n in ("hi", "lo")]
            work = Ring(self.sbs(scope, "f_work", 2, [P, T]))
            lows = Ring(self.sbs(scope, "f_lows", 2, [P, DK, P], F32R))
            self.low_n = 0

            def low_products(name, cols, ready, products):
                n_in = shapes[name][1] // P
                low = lows.take()
                stream = self.stream(f"f_low{low.index}")
                sp.need(low.free)
                stream.count += 16
                with nc.If(wider != 0):
                    sp.q.dma_start(low.ap[:, 0:n_in, :].bitcast(F32), lo_dram[name][:, :, cols]).then_inc(stream.sem, 16)
                    pe.q.wait_ge(stream.sem, stream.count)
                    products(low.ap)
                with nc.Else():
                    sp.q.sem_inc(stream.sem, 16)
                return low

            def linear_T(name, m, src, ready, ps):
                cols = slice(m * P, (m + 1) * P)
                n_in = shapes[name][1] // P
                w = W[name]
                pe.need(ready, ps.free)
                self.product(ps.ap, [(w[:, k, cols], src[0][:, k, :]) for k in range(n_in)], stop=False)
                low = low_products(name, cols, ready, lambda l: self.product(
                    ps.ap, [(l[:, k, :], src[0][:, k, :]) for k in range(n_in)], start=False, stop=False))
                done = pe.mark(self.product(ps.ap, [(w[:, k, cols], src[1][:, k, :]) for k in range(n_in)], start=False))
                release(low, done)
                return done

            loaded, keep = {}, {}

            def load(g):
                x = x_ring.take()
                sp.need(x.free)
                loaded[g] = (x, self.stream(f"f_x{x.index}").start(sp, x.ap, self.x3[g].rearrange("(t p) c -> p t c", p=P)))

            def prepare(g):
                x, m_x = loaded[g]
                m_norm = self.norm(x.ap, xn, stats, m_x, keep.get("xn_free"))
                hi, lo = xT[0].take(), xT[1].take()
                ready = self.transposed(xn, hi.ap, lo.ap, banks, m_norm, [hi.free, lo.free])
                keep["xn_free"] = [(pe.sem, pe.count)]
                keep[g] = (hi, lo, ready)

            def group(g):
                x, _ = loaded[g]
                hi, lo, ready = keep[g]
                src, src_slots = (hi.ap, lo.ap), (hi, lo)
                out = (hs[0].take(), hs[1].take())
                marks = []
                for m in range(DK):
                    pa, pb = banks.take(), banks.take()
                    da = linear_T("w1", m, src, ready, pa)
                    db = linear_T("w2", m, src, ready, pb)
                    w = work.take()
                    act.need(da, w.free)
                    ms = act.mark(nc.scalar.activation(w.ap, pa.ap, ACT.Silu, scale=S["w1"][:, m:m + 1]))
                    release(pa, ms)
                    dve.need(ms, db)
                    mh = dve.mark(nc.vector.scalar_tensor_tensor(out=w.ap, in0=pb.ap, scalar=S["w2"][:, m:m + 1], in1=w.ap,
                                                                 op0=ALU.mult, op1=ALU.mult))
                    release(pb, mh)
                    act.need(mh, out[0].free)
                    m1 = act.mark(nc.scalar.activation(out[0].ap[:, m, :], w.ap, ACT.Copy))
                    dve.need(m1, out[1].free)
                    m2 = dve.mark(nc.vector.tensor_tensor(out[1].ap[:, m, :], w.ap, out[0].ap[:, m, :].bitcast(F32), ALU.subtract))
                    release(w, m2)
                    marks += [m1, m2]
                for s in src_slots:
                    release(s, (pe.sem, pe.count))
                if g + 1 < B:
                    prepare(g + 1)
                for name in ("h1", "h2"):
                    src, src_slots, ready = (out[0].ap, out[1].ap), out, marks
                    out = (hs[0].take(), hs[1].take())
                    marks = []
                    for m in range(DK):
                        ps = banks.take()
                        done = linear_T(name, m, src, ready, ps)
                        w = work.take()
                        act.need(done, w.free)
                        ms = act.mark(nc.scalar.activation(w.ap, ps.ap, ACT.Gelu, scale=S[name][:, m:m + 1]))
                        release(ps, ms)
                        dve.need(ms, out[0].free, out[1].free)
                        m1 = dve.mark(nc.vector.tensor_copy(out[0].ap[:, m, :], w.ap))
                        dve.need(m1)
                        m2 = dve.mark(nc.vector.tensor_tensor(out[1].ap[:, m, :], w.ap, out[0].ap[:, m, :].bitcast(F32), ALU.subtract))
                        release(w, m2)
                        marks += [m2]
                    for s in src_slots:
                        release(s, (pe.sem, pe.count))
                src = (out[0].ap, out[1].ap)
                for half in range(CK):
                    cols = slice(half * P, (half + 1) * P)
                    ps = banks.take()
                    pe.need(marks, ps.free)
                    w = W["w3"]
                    tiles = [(ps.ap[:, t * P:(t + 1) * P], slice(t * P, (t + 1) * P)) for t in range(NT)]
                    for n, (o, toks) in enumerate(tiles):
                        self.product(o, [(src[0][:, k, toks], w[:, k, cols]) for k in range(DK)],
                                     start=n == 0, stop=False, skip_group_check=True)

                    def third(l):
                        for o, toks in tiles:
                            self.product(o, [(src[0][:, k, toks], l[:, k, :]) for k in range(DK)],
                                         start=False, stop=False, skip_group_check=True)
                    low = low_products("w3", cols, marks, third)
                    for o, toks in tiles:
                        last = self.product(o, [(src[1][:, k, toks], w[:, k, cols]) for k in range(DK)],
                                            start=False, skip_group_check=True)
                    done = pe.mark(last)
                    release(low, done)
                    wk = work.take()
                    dve.need(done, wk.free)
                    v = ps.ap.rearrange("p (t c) -> p t c", t=NT)
                    m = dve.mark(nc.vector.tensor_tensor(wk.ap.rearrange("p (t c) -> p t c", t=NT), v,
                                                         s3[:, cols].unsqueeze(1).to_broadcast([P, NT, P]), ALU.mult))
                    release(ps, m)
                    pool.need(m)
                    part = x.ap[:, :, cols]
                    m = pool.mark(nc.gpsimd.tensor_tensor(part, part, wk.ap.rearrange("p (t c) -> p t c", t=NT), ALU.add))
                    release(wk, m)
                for s in out:
                    release(s, done)
                sp.need(m)
                m = self.stream(f"f_out{x.index}").start(sp, self.out[g].rearrange("(t p) c -> p t c", p=P), x.ap)
                release(x, m)
                if g + 2 < B:
                    load(g + 2)

            load(0)
            load(1)
            prepare(0)
            for g in range(B):
                group(g)
            self.barrier()

    def build(self):
        with ExitStack() as scope:
            self.constants(scope)
            self.attention(0)
            self.route_and_share(scope)
            self.experts()
            self.attention(1)
            self.feed_forward()
            self.barrier()


def kernel(**inputs):
    import numpy as np
    import concourse.bacc as bacc
    from concourse.bass_utils import run_bass_kernel_spmd

    nc = bacc.Bacc("TRN2", target_bir_lowering=False, num_devices=1)
    arrays, args = {}, {}
    for name, value in inputs.items():
        a = np.ascontiguousarray(value)
        arrays[f"in_{name}"] = a
        args[name] = nc.dram_tensor(f"in_{name}", a.shape, mybir.dt.from_np(a.dtype), kind="ExternalInput").ap()
    out = nc.dram_tensor("out_x", (B, T, C), F32, kind="ExternalOutput").ap()
    Program(nc, args, out).build()
    r = run_bass_kernel_spmd(nc, [arrays], core_ids=[0])
    return r.results[0]["out_x"]
```

```python
from contextlib import ExitStack

import concourse.bass as bass
import concourse.mybir as mybir

F32 = mybir.dt.float32
F32R = mybir.dt.float32r
BF16 = mybir.dt.bfloat16
I32 = mybir.dt.int32
ALU = mybir.AluOpType
ACT = mybir.ActivationFunctionType
AXIS = mybir.AxisListType.X

P = 128
B, T, C = 16, 512, 256
TC, CC = 64, 128
H, DH = 16, 16
E, HID = 32, 512
DH1 = 1024
NT = T // P
CK = C // P
QUADS = H // 4
NTILES = B * NT
SLOTS = NTILES + E - 1
HK = HID // P
DK = DH1 // P
EPS = 1e-5
SCALE = 1.0 / DH ** 0.5
MASKED = -1e30
ROWS = 4 * DH
KROWS = ROWS + 2
VW = 32


def flat(marks):
    for m in marks:
        if m is None:
            continue
        if isinstance(m, list):
            yield from flat(m)
        else:
            yield m


class Engine:

    def __init__(self, nc, queue, name, serial=False):
        self.q, self.name, self.serial = queue, name, serial
        self.sem = nc.alloc_semaphore(f"{name}_done")
        self.count = 0
        self.waited = {}

    def mark(self, instruction):
        instruction.then_inc(self.sem, 1)
        self.count += 1
        if self.serial:
            self.need((self.sem, self.count))
        return (self.sem, self.count)

    def need(self, *marks):
        for sem, value in flat(marks):
            if self.waited.get(sem.name, 0) < value:
                self.waited[sem.name] = value
                self.q.wait_ge(sem, value)


class Stream:

    def __init__(self, nc, name):
        self.sem = nc.alloc_semaphore(f"{name}_dma")
        self.count = 0

    def start(self, engine, out, in_, **how):
        engine.q.dma_start(out, in_, **how).then_inc(self.sem, 16)
        self.count += 16
        return (self.sem, self.count)

    def last(self):
        return (self.sem, self.count)


class Slot:
    def __init__(self, ap, index):
        self.ap, self.index, self.free, self.held, self.hi = ap, index, None, False, None


class Ring:

    def __init__(self, aps):
        self.slots = [Slot(a, i) for i, a in enumerate(aps)]
        self.n = 0

    def take(self):
        s = self.slots[self.n % len(self.slots)]
        assert not s.held
        s.held = True
        self.n += 1
        return s


def release(slot, *marks):
    slot.free = list(marks)
    slot.held = False


class Plan:

    def __init__(self):
        self.waiting = []

    def add(self, start, span, steps, generator):
        self.waiting.append([start, len(self.waiting), span / steps, generator])

    def run(self):
        while self.waiting:
            entry = min(self.waiting, key=lambda e: e[:2])
            for _ in entry[3]:
                entry[0] += entry[2]
                break
            else:
                self.waiting.remove(entry)


class Temporary(ExitStack):
    pass


class Program:
    def __init__(self, nc, inp, out):
        self.nc, self.inp, self.out = nc, inp, out
        self.pe = Engine(nc, nc.tensor, "pe")
        self.act = Engine(nc, nc.scalar, "act")
        self.dve = Engine(nc, nc.vector, "dve")
        self.pool = Engine(nc, nc.gpsimd, "pool", serial=True)
        self.sp = Engine(nc, nc.sync, "sp")
        self.engines = [self.pe, self.act, self.dve, self.pool, self.sp]
        self.streams = {}
        self.x1 = nc.dram_tensor("x_after_attention0", [B, T, C], F32).ap()
        self.x2 = nc.dram_tensor("x_after_shared0", [B, T, C], F32).ap()
        self.x3 = nc.dram_tensor("x_after_attention1", [B, T, C], F32).ap()
        self.sorted_x = nc.dram_tensor("sorted_x", [SLOTS * P, C], F32).ap()
        self.sorted_y = nc.dram_tensor("sorted_y", [SLOTS * P, C], F32).ap()
        self.psum = nc.alloc_psum_tensor("psum", [P, 8 * 512], F32).ap()

    def stream(self, name):
        if name not in self.streams:
            self.streams[name] = Stream(self.nc, name)
        return self.streams[name]

    def bank(self, i, n=1):
        return self.psum[:, i * 512:(i + n) * 512]

    def sb(self, scope, name, shape, dt=F32):
        side = "right" if isinstance(scope, Temporary) else "left"
        return scope.enter_context(self.nc.sbuf_tensor(name, shape, dt, side=side)).ap()

    def sbs(self, scope, name, n, shape, dt=F32):
        return [self.sb(scope, f"{name}{i}", shape, dt) for i in range(n)]

    def barrier(self, but=()):
        marks = [(e.sem, e.count) for e in self.engines if e.count]
        marks += [s.last() for name, s in self.streams.items() if name not in but]
        for e in self.engines:
            e.need(marks)

    def split_psum(self, src, hi, lo, needs, free, bias=None):
        self.act.need(needs, free)
        if bias is None:
            m_hi = self.act.mark(self.nc.scalar.activation(hi, src, ACT.Copy))
        else:
            m_hi = self.act.mark(self.nc.scalar.activation(hi, src, ACT.Identity, bias=bias))
        self.dve.need(m_hi, free)
        if bias is None:
            m_lo = self.dve.mark(self.nc.vector.tensor_tensor(lo, src, hi.bitcast(F32), ALU.subtract))
        else:
            m_lo = self.dve.mark(self.nc.vector.scalar_tensor_tensor(
                out=lo, in0=src, scalar=bias, in1=hi.bitcast(F32), op0=ALU.add, op1=ALU.subtract))
        return [m_hi, m_lo]

    def split_sbuf(self, src, hi, lo, needs):
        self.dve.need(needs)
        m = self.dve.mark(self.nc.vector.tensor_copy(hi, src))
        self.dve.need(m)
        return self.dve.mark(self.nc.vector.tensor_tensor(lo, src, hi.bitcast(F32), ALU.subtract))

    def product(self, out, pairs, start=True, stop=True, **how):
        for n, (lhsT, rhs) in enumerate(pairs):
            last = self.nc.tensor.matmul(out, lhsT, rhs, start=start and n == 0, stop=stop and n == len(pairs) - 1, **how)
        return last

    def constants(self, scope):
        nc, pool, dve, act = self.nc, self.pool, self.dve, self.act
        self.ident = self.sb(scope, "ident", [P, P])
        self.ident16 = self.sb(scope, "ident16", [P, P], BF16)
        self.mask_qk = self.sb(scope, "mask_qk", [P, 2 * P], BF16)
        self.before = self.sb(scope, "before", [P, P], BF16)
        self.ones16 = self.sb(scope, "ones16", [P, P], BF16)
        self.ones = self.sb(scope, "ones", [P, P])
        self.half = self.sb(scope, "minus_half", [P, NT])
        self.gate = self.sb(scope, "gate", [P, 4])
        for t, v in ((self.ident, 0.0), (self.ident16, 0.0), (self.mask_qk, 0.0),
                     (self.before, 0.0), (self.ones16, 1.0), (self.ones, 1.0), (self.half, -0.5)):
            m = pool.mark(nc.gpsimd.memset(t, v))
        pool.need(m)

        def select(t, op, fill, step, per_partition):
            nc_i = nc.gpsimd.affine_select(out=t, in_=t, compare_op=op, fill=fill, base=0,
                                           pattern=[[step, P]], channel_multiplier=per_partition)
            return pool.mark(nc_i)
        select(self.ident, ALU.not_equal, 1.0, -1, 1)
        select(self.ident16, ALU.not_equal, 1.0, -1, 1)
        select(self.mask_qk[:, P:], ALU.is_ge, MASKED, -1, 1)
        made = select(self.before, ALU.is_ge, 1.0, -1, 1)
        raw = self.sb(scope, "gate_raw", [P, 4])
        s = self.stream("setup")
        s.start(self.sp, raw[:, 0:2], self.inp["g_xattn"].partition_broadcast(P))
        m = s.start(self.sp, raw[:, 2:4], self.inp["g_ffn"].partition_broadcast(P))
        act.need(m)
        m = act.mark(nc.scalar.activation(self.gate, raw, ACT.Tanh))
        for e in (self.pe, self.dve, self.act, self.pool, self.sp):
            e.need(made, m)

    def norm(self, x, y, stats, needs, free):
        for step in self.norm_steps(x, y, stats, needs, free):
            pass
        return step

    def norm_steps(self, x, y, stats, needs, free):
        nc, dve, pool = self.nc, self.dve, self.pool
        dve.need(needs, free)
        for t in range(NT):
            m = dve.mark(nc.vector.bn_stats(stats["raw"][:, t, :], x[:, t, :]))
        dve.need(m)
        for t in range(NT):
            m = dve.mark(nc.vector.bn_aggr(stats["mv"][:, t, :], stats["raw"][:, t, :]))
        dve.need(m)
        m = dve.mark(nc.vector.tensor_scalar(stats["var"], stats["mv"][:, :, 1], EPS, None, ALU.add))
        pool.need(m)
        m = pool.mark(nc.gpsimd.tensor_tensor(stats["rstd"], stats["var"], self.half, ALU.pow))
        yield
        dve.need(m)
        for t in range(NT):
            m = dve.mark(nc.vector.tensor_scalar(y[:, t, :], x[:, t, :], stats["mv"][:, t, 0:1],
                                                 stats["rstd"][:, t:t + 1], ALU.subtract, ALU.mult))
        yield m

    def norm_scratch(self, scope, name):
        return {"raw": self.sb(scope, f"{name}_raw", [P, NT, 6]), "mv": self.sb(scope, f"{name}_mv", [P, NT, 2]),
                "var": self.sb(scope, f"{name}_var", [P, NT]), "rstd": self.sb(scope, f"{name}_rstd", [P, NT])}

    def transposed(self, x, hi, lo, banks, needs, free):
        marks = []
        for c in range(CK):
            ps = banks.take()
            self.pe.need(needs, ps.free)
            for t in range(NT):
                last = self.nc.tensor.transpose(ps.ap[:, t * P:(t + 1) * P], x[:, t, c * P:(c + 1) * P], self.ident)
            m = self.split_psum(ps.ap, hi[:, c, :], lo[:, c, :], self.pe.mark(last), free)
            release(ps, *m)
            marks += m
        return marks

    def load_split(self, scope, name, dram, chunks, width, stage, permute=False, twice=False):
        copies = 2 if twice else 1
        hi = self.sb(scope, f"{name}_hi", [P, chunks, copies * width], F32R)
        lo = self.sb(scope, f"{name}_lo", [P, chunks, copies * width], F32R)
        st = stage.take()
        view = st.ap[:, 0:chunks * width]
        self.sp.need(st.free)
        m = self.stream(f"weights{st.index}").start(
            self.sp, view.rearrange("p (c n) -> p c n", c=chunks), dram.rearrange("(c p) n -> p c n", p=P))
        if not permute:
            v = view.rearrange("p (c n) -> p c n", c=chunks)
            m = self.split_sbuf(v, hi, lo, m)
        else:
            for c in range(chunks):
                src = st.ap[:, c * width:(c + 1) * width].rearrange("p (q h d) -> p q d h", h=4, d=DH)
                for copy in range(copies):
                    def dst(t):
                        return t[:, c, :].rearrange("p (q r d h) -> p q r d h", r=copies, h=4, d=DH)[:, :, copy]
                    m = self.split_sbuf(src, dst(hi), dst(lo), m)
        release(st, m)
        return {"hi": hi, "lo": lo, "ready": m}

    def load_bias_column(self, scope, name, dram, queue):
        t = self.sb(scope, name, [P, CK])
        s = self.stream(name)
        v = dram.rearrange("(c q h d) -> c q d h", q=2, h=4, d=DH)
        for c in range(CK):
            for q in range(2):
                m = s.start(queue, t[64 * q:64 * q + 64, c:c + 1], v[c, q], allow_slow_non_contiguous=True)
        return t, m

    def load_bias_twice(self, scope, name, dram, queue):
        t = self.sb(scope, name, [P, QUADS])
        s = self.stream(name)
        v = dram.rearrange("(q h d) -> q d h", h=4, d=DH)
        for q in range(QUADS):
            for r in range(2):
                m = s.start(queue, t[64 * r:64 * r + 64, q:q + 1], v[q], allow_slow_non_contiguous=True)
        return t, m

    def load_row(self, scope, name, dram):
        t = self.sb(scope, name, [P, dram.shape[0]])
        m = self.stream(name).start(self.sp, t, dram.partition_broadcast(P))
        return t, m

    def context(self, scope, banks, pre):
        nc = self.nc
        hi = self.sb(scope, pre + "ctx_hi", [P, B, TC], F32R)
        lo = self.sb(scope, pre + "ctx_lo", [P, B, TC], F32R)
        with Temporary() as tmp:
            raw = self.sb(tmp, pre + "ctx_raw", [P, B // 2, CC])
            m = self.stream("ctx").start(self.sp, raw, self.inp["ctx_512"].rearrange("(a b) t c -> (b t) a c", b=2))
            per = min(B, 8)
            for g in range(B // per):
                ps = banks.take()
                self.pe.need(m, ps.free)
                for j in range(per // 2):
                    last = nc.tensor.transpose(ps.ap[:, j * P:(j + 1) * P], raw[:, per // 2 * g + j, :], self.ident)
                done = self.pe.mark(last)
                src = ps.ap[:, 0:per * TC].rearrange("p (b t) -> p b t", t=TC)
                marks = self.split_psum(src, hi[:, per * g:per * (g + 1), :], lo[:, per * g:per * (g + 1), :], done, None)
                release(ps, *marks)
            self.barrier(but=("scatter",))
        return {"hi": hi, "lo": lo}

    def attention_weights(self, layer, scope):
        nc, dve, sp = self.nc, self.dve, self.sp
        own = layer == 0
        inp = self.inp
        pre = f"L{layer}_xattn_"
        L = f"a{layer}_"
        banks = Ring([self.bank(6), self.bank(7)])
        names = (dict(q="Wq", k="Wk", v="Wv", cq="Wcq", ck="Wck", cv="Wcv", o="Wp") if own
                 else dict(cq="Wq", ck="Wk", cv="Wv", o="Wo"))
        biases = {k: "b" + v[1:] for k, v in names.items()}
        W = {}
        with Temporary() as tmp:
            stage = Ring(self.sbs(tmp, L + "wstage", 2, [P, 2 * C]))
            for k in ("cq", "q", "k", "v", "cv", "ck", "o"):
                if k in names:
                    chunks = 1 if k in ("ck", "cv") else CK
                    W[k] = self.load_split(scope, L + "w" + k, inp[pre + names[k]], chunks, C, stage, permute=k in ("cq", "q", "k", "ck"),
                                           twice=k in ("cq", "ck"))
            bias_col, bias_row = {}, {}
            for k in ("q", "k", "cq", "ck"):
                if k in names:
                    bias = self.load_bias_twice if k in ("cq", "ck") else self.load_bias_column
                    bias_col[k] = bias(scope, L + "b" + k, inp[pre + biases[k]], self.pool if own else sp)
            for k in ("v", "cv", "o"):
                if k in names:
                    bias_row[k] = self.load_row(scope, L + "b" + k, inp[pre + biases[k]])
            gate = self.gate[:, layer:layer + 1]
            ob, ready = bias_row["o"]
            dve.need(ready)
            dve.mark(nc.vector.tensor_scalar(ob, ob, gate, None, ALU.mult))
            ctx = self.context(tmp, banks, L)
            ctx_dram = nc.dram_tensor(L + "ctx_halves", [2, P, B * TC], F32).ap()
            for n, x in enumerate(("hi", "lo")):
                self.stream("setup").start(sp, ctx_dram[n], ctx[x].rearrange("p b t -> p (b t)").bitcast(F32))
            self.barrier(but=("scatter",))
        return W, bias_col, bias_row, ctx_dram

    def attention(self, layer, W, bias_col, bias_row, ctx_dram):
        nc, pe, act, dve, pool, sp = self.nc, self.pe, self.act, self.dve, self.pool, self.sp
        own = layer == 0
        inp = self.inp
        with ExitStack() as scope:
            L = f"a{layer}_"
            gate = self.gate[:, layer:layer + 1]
            ob, _ = bias_row["o"]
            n_score, n_prob, n_value = (3, 2, 1) if own else (2, 2, 1)
            free_banks = iter(range(8))
            score_banks, prob_banks, value_banks = (Ring([self.bank(next(free_banks)) for _ in range(n)])
                                                    for n in (n_score, n_prob, n_value))
            banks = Ring([self.bank(i) for i in free_banks])
            own_heads = 4 if own else 0
            nq = own_heads + 4
            x_ring = Ring(self.sbs(scope, L + "x", 1 if own else 2, [P, NT, C]))
            residual = Ring(self.sbs(scope, L + "residual", 1, [P, NT, C]))
            xn = self.sb(scope, L + "xn", [P, NT, C])
            QN = Ring(self.sbs(scope, L + "QN", 9 if own else 12, [P, T], F32R))
            KB = Ring(self.sbs(scope, L + "KB", 2 if own else 3, [P, QUADS, 2, 4, TC], F32R))
            keys = self.sb(scope, L + "keys", [P, QUADS, TC])
            key_halves = self.sb(scope, L + "key_halves", [P, 2, QUADS, TC], F32R)
            cross_max = Ring(self.sbs(scope, L + "cross_max", 2 if own else 3, [P, T], F32R))
            chosen = self.sb(scope, L + "chosen", [P, 2, P], F32R)
            row_head = self.sb(scope, L + "row_head", [P, 4])
            ctx_twice = self.sb(scope, L + "ctx_twice", [P, 2, 2, TC], F32R)
            stats = self.norm_scratch(scope, L + "ln")
            xT_hi = self.sb(scope, L + "xT_hi", [P, CK, T], F32R)
            xT_lo = self.sb(scope, L + "xT_lo", [P, CK, T], F32R)
            stage = Ring(self.sbs(scope, L + "stage", 3, [P, 2, T], F32R))
            if own:
                Q = Ring(self.sbs(scope, L + "Q", 3, [KROWS, 4, T], F32R))
                K = Ring(self.sbs(scope, L + "K", 3, [KROWS, 4, T], F32R))
                V = Ring(self.sbs(scope, L + "V", 2, [P, NT, H, VW]))
            VC = Ring(self.sbs(scope, L + "VC", 2 if own else 4, [P, H, VW]))
            probs = Ring(self.sbs(scope, L + "probs", 7 if own else 8, [P, T]))
            maxima = Ring(self.sbs(scope, L + "maxima", 2 if own else 5, [P, nq, NT]))
            minus_max = Ring(self.sbs(scope, L + "minus_max", 2, [16, 2, P], F32R)) if own else None
            ysum = Ring(self.sbs(scope, L + "ysum", 1 if own else 2, [P, T]))
            recip = Ring(self.sbs(scope, L + "recip", 2 if own else 3, [P, 2, NT, 4]))
            ycross = self.sb(scope, L + "ycross", [P, NT, 4, DH])
            Y = Ring(self.sbs(scope, L + "Y", 2, [P, NT, C]))

            made = []
            if own:
                for s in K.slots:
                    made.append(dve.mark(nc.vector.memset(s.ap[ROWS:KROWS].bitcast(F32), 1.0)))
            made.append(dve.mark(nc.vector.tensor_reduce(row_head, self.ident.rearrange("p (j h) -> p h j", h=4), AXIS, ALU.max)))
            for h in range(4):
                made.append(dve.mark(nc.vector.tensor_tensor(
                    chosen[:, h // 2, (h % 2) * TC:(h % 2 + 1) * TC], self.ident[:, h:h + 1].to_broadcast([P, TC]),
                    self.ident[:, 32 + h:33 + h].to_broadcast([P, TC]), ALU.add)))
            for s in cross_max.slots:
                made.append(dve.mark(nc.vector.memset(s.ap.bitcast(F32), 0.0)))
            values = (list(V.slots) if own else []) + list(VC.slots)
            for s in values:
                m = pool.mark(nc.gpsimd.memset(s.ap, 0.0))
                pool.need(m)
                a = s.ap
                if s in VC.slots:
                    for r in range(2):
                        made.append(pool.mark(nc.gpsimd.memset(a[r * TC:(r + 1) * TC, r::2, DH:DH + 1], 1.0)))
                else:
                    made.append(pool.mark(nc.gpsimd.memset(a[:, :, :, DH:DH + 1], 1.0)))
            if own:
                zero_rows = nc.dram_tensor(L + "zero_rows", [2, 4 * T], F32).ap()
                m = pool.mark(nc.gpsimd.memset(xn, 0.0))
                sp.need(m)
                made.append(self.stream("setup").start(
                    sp, zero_rows.rearrange("a (b n) -> (a b) n", n=1024), xn.rearrange("p t c -> p (t c)")[0:2 * 4 * T // 1024, :]))
            for e in self.engines:
                e.need(made)
                sorted_rows = self.sorted_x.rearrange("(r a) c -> r (a c)", a=4 * T // C)
                zero_part = -(-SLOTS * P * C // (4 * T) // B)
            scratch = {}
            for k in ("q", "k"):
                if own:
                    scratch[k] = nc.dram_tensor(f"{L}{k}_packed", [B, 2, C, T], F32).ap()
            x_in = inp["x"] if own else self.x2
            x_out = self.x1 if own else self.x3
            state = {b: {} for b in range(B)}
            unit = {u: {} for u in range(B * QUADS)}
            if not own:
                gathered = Ring(self.sbs(scope, L + "gathered", 2, [P, NT, C]))

            def prepare(b):
                st = state[b]
                sp.need(state.get("twice_free"))
                for n in range(2):
                    twice_ready = self.stream("ctx_twice").start(
                        sp, ctx_twice[:, n, :, :].bitcast(F32),
                        ctx_dram[n, :, b * TC:(b + 1) * TC].unsqueeze(1).to_broadcast([P, 2, TC]))
                xs = x_ring.take()
                sp.need(xs.free)
                m = self.stream(f"x{xs.index}").start(sp, xs.ap, x_in[b].rearrange("(t p) c -> p t c", p=P))
                if not own:
                    g = gathered.take()
                    pool.need(g.free)
                    s = self.stream(f"gather{g.index}")
                    for t in range(NT):
                        nc.gpsimd.indirect_dma_start(
                            out=g.ap[:, t, :], out_offset=None, in_=self.sorted_y[:],
                            in_offset=bass.IndirectOffsetOnAxis(ap=self.position[:, b * NT + t:b * NT + t + 1], axis=0)
                        ).then_inc(s.sem, 16)
                        s.count += 16
                    yield
                    dve.need(m, s.last())
                    m = dve.mark(nc.vector.scalar_tensor_tensor(
                        out=xs.ap, in0=g.ap, scalar=self.gate[:, 2:3], in1=xs.ap, op0=ALU.mult, op1=ALU.add))
                    release(g, m)
                yield
                steps = self.norm_steps(xs.ap, xn, stats, m, state.get("xn_free"))
                next(steps)
                yield
                m_norm = next(steps)
                pool.need(m_norm)
                m = pool.mark(nc.gpsimd.tensor_tensor(xs.ap, xs.ap, ob.unsqueeze(1).to_broadcast([P, NT, C]), ALU.add))
                sp.need(m)
                st["x_kept"] = self.stream("x_kept").start(sp, x_out[b].rearrange("(t p) c -> p t c", p=P), xs.ap)
                release(xs, st["x_kept"])
                yield
                xT = self.transposed(xn, xT_hi, xT_lo, banks, m_norm, state.get("xT_free"))
                state["xn_free"] = [(pe.sem, pe.count)]
                halves = {"hi": xT_hi, "lo": xT_lo}
                yield
                for k in ("q", "k"):
                    if not own:
                        continue
                    w, (bias, bias_ready) = W[k], bias_col[k]
                    both = []
                    for c in range(CK):
                        ps = banks.take()
                        pe.need(xT, w["ready"], ps.free)
                        pairs = [(w[a][:, kc, c * P:(c + 1) * P], halves[x][:, kc, :])
                                 for a, x in (("hi", "hi"), ("lo", "hi"), ("hi", "lo")) for kc in range(CK)]
                        both.append([c, ps, pe.mark(self.product(ps.ap, pairs)), stage.take()])
                    for c, ps, done, s in both:
                        act.need(done, bias_ready, s.free)
                        s.hi = act.mark(nc.scalar.activation(s.ap[:, 0, :], ps.ap, ACT.Identity, bias=bias[:, c:c + 1]))
                    for c, ps, done, s in both:
                        dve.need(s.hi)
                        m = dve.mark(nc.vector.scalar_tensor_tensor(
                            out=s.ap[:, 1, :], in0=ps.ap, scalar=bias[:, c:c + 1], in1=s.ap[:, 0, :].bitcast(F32),
                            op0=ALU.add, op1=ALU.subtract))
                        release(ps, m)
                        sp.need(m)
                        m = self.stream(f"stage{s.index}").start(
                            sp, scratch[k][b, :, c * P:(c + 1) * P, :].rearrange("k r n -> r k n"), s.ap.bitcast(F32))
                        release(s, m)
                        st.setdefault("packed", []).append(m)
                    yield
                w, (bias, bias_ready) = W["cq"], bias_col["cq"]
                for q0 in range(0, QUADS, 2):
                    both = []
                    for quad in (q0, q0 + 1):
                        ps = banks.take()
                        pe.need(xT, w["ready"], ps.free)
                        done = pe.mark(self.product(ps.ap, [
                            (w[a][:, kc, quad * P:(quad + 1) * P], halves[x][:, kc, :])
                            for a, x in (("hi", "hi"), ("lo", "hi"), ("hi", "lo")) for kc in range(CK)]))
                        both.append((quad, ps, done, QN.take()))
                    for quad, ps, done, qn in both:
                        act.need(done, bias_ready, qn.free)
                        qn.hi = act.mark(nc.scalar.activation(qn.ap, ps.ap, ACT.Identity, bias=bias[:, quad:quad + 1]))
                    for quad, ps, done, qn in both:
                        dve.need(qn.hi)
                        low = qn.ap[64:P, :]
                        m_lo = dve.mark(nc.vector.scalar_tensor_tensor(
                            out=low, in0=ps.ap[64:P, :], scalar=bias[64:P, quad:quad + 1], in1=low.bitcast(F32),
                            op0=ALU.add, op1=ALU.subtract))
                        release(ps, m_lo)
                        unit[QUADS * b + quad].update(QN=qn, QN_ready=[qn.hi, m_lo])
                    yield
                if own:
                    st["V"] = v = V.take()
                    bias, bias_ready = bias_row["v"]
                    for half in range(2):
                        ps = banks.take()
                        pe.need(xT, W["v"]["ready"], ps.free)
                        for j in range(2):
                            t = 2 * half + j
                            pairs = [(halves[x][:, kc, t * P:(t + 1) * P], W["v"][a][:, kc, :])
                                     for x, a in (("hi", "hi"), ("lo", "hi"), ("hi", "lo")) for kc in range(CK)]
                            last = self.product(ps.ap[:, j * C:(j + 1) * C], pairs)
                        dve.need(pe.mark(last), bias_ready, v.free)
                        m = dve.mark(nc.vector.tensor_tensor(
                            v.ap[:, 2 * half:2 * half + 2, :, 0:DH],
                            ps.ap.rearrange("p (t h d) -> p t h d", t=2, d=DH),
                            bias.rearrange("p (h d) -> p h d", d=DH).unsqueeze(1).to_broadcast([P, 2, H, DH]), ALU.add))
                        release(ps, m)
                        yield
                    st["V_ready"] = m
                if own:
                    part = sorted_rows[b * zero_part:min((b + 1) * zero_part, sorted_rows.shape[0])]
                    self.stream("zero_sorted").start(sp, part, zero_rows[0:1, :].to_broadcast([part.shape[0], 4 * T]))
                state["xT_free"] = [(pe.sem, pe.count)]
                st["VC"] = v = VC.take()
                bias, bias_ready = bias_row["cv"]
                ps = banks.take()
                pe.need(twice_ready, W["cv"]["ready"], ps.free)
                twice = {x: ctx_twice[:, n, :, :].rearrange("p r t -> p (r t)") for n, x in enumerate(("hi", "lo"))}
                pairs = [(twice[x], W["cv"][a][:, 0, :]) for x, a in (("hi", "hi"), ("lo", "hi"), ("hi", "lo"))]
                dve.need(pe.mark(self.product(ps.ap[:, 0:C], pairs)), bias_ready, v.free)
                state["twice_free"] = (pe.sem, pe.count)
                for r in range(2):
                    rows = slice(r * TC, (r + 1) * TC)
                    m = dve.mark(nc.vector.tensor_tensor(
                        v.ap[rows, r::2, 0:DH], ps.ap[rows, 0:C].rearrange("p (h d) -> p h d", d=DH)[:, r::2, :],
                        bias[rows].rearrange("p (h d) -> p h d", d=DH)[:, r::2, :], ALU.add))
                release(ps, m)
                st["VC_ready"] = m
                ps = banks.take()
                bias, bias_ready = bias_col["ck"]
                pe.need(W["ck"]["ready"], ps.free)
                w = W["ck"]
                for quad in range(QUADS):
                    last = self.product(ps.ap[:, quad * TC:(quad + 1) * TC], [
                        (w[a][:, 0, quad * P:(quad + 1) * P], ctx_twice[:, x, 0, :]) for a, x in (("hi", 0), ("lo", 0), ("hi", 1))])
                done = pe.mark(last)
                state["twice_free"] = done
                dve.need(done, bias_ready)
                m = dve.mark(nc.vector.tensor_tensor(keys, ps.ap[:, 0:QUADS * TC].rearrange("p (q n) -> p q n", n=TC),
                                                     bias.unsqueeze(2).to_broadcast([P, QUADS, TC]), ALU.add))
                release(ps, m)
                dve.need(m)
                m = dve.mark(nc.vector.tensor_copy(key_halves[:, 0], keys))
                dve.need(m)
                m = dve.mark(nc.vector.tensor_tensor(key_halves[:, 1], keys, key_halves[:, 0].bitcast(F32), ALU.subtract))
                st["KB"] = kb = KB.take()
                dve.need(m, kb.free)
                for half in range(2):
                    m = dve.mark(nc.vector.tensor_tensor(
                        kb.ap[:, :, half], key_halves[:, half].bitcast(F32).unsqueeze(2).to_broadcast([P, QUADS, 4, TC]),
                        row_head.unsqueeze(1).unsqueeze(3).to_broadcast([P, QUADS, 4, TC]), ALU.mult))
                st["KB_ready"] = m
                yield

            def pack(u):
                b, quad = divmod(u, QUADS)
                un, rows = unit[u], slice(64 * quad, 64 * quad + 64)
                un["Q"] = q = Q.take()
                sp.need(state[b]["packed"], q.free)
                s = self.stream(f"pack_q{q.index}")
                m = None
                src = scratch["q"][b, :, rows, :].rearrange("k (d h) n -> k d (h n)", h=4)
                for rep in range(2):
                    s.start(sp, q.ap[rep * 2 * DH:(rep + 1) * 2 * DH].bitcast(F32), src)
                un["ready"] = [s.start(sp, q.ap[ROWS:KROWS].bitcast(F32), zero_rows)]
                un["K"] = k_ = K.take()
                sp.need(k_.free)
                src = scratch["k"][b, :, rows, :].rearrange("k (d h) n -> k d (h n)", h=4)
                for half in range(2):
                    m = self.stream(f"pack_k{k_.index}").start(
                        sp, k_.ap[half * 2 * DH:(half + 1) * 2 * DH].bitcast(F32),
                        src[half].unsqueeze(0).to_broadcast([2, DH, 4 * T]))
                un["ready"].append(m)
                yield

            def find_max(u):
                b, quad = divmod(u, QUADS)
                un, st = unit[u], state[b]
                q = un["Q"].ap if own else None
                mx = maxima.take()
                dve.need(mx.free)
                tasks = []
                if own:
                    tasks += [(3, [h]) for h in range(4)] + [(2, [h]) for h in range(4)]
                    tasks += [(1, [0, 1]), (1, [2, 3]), (0, [0, 1, 2, 3])]
                c0 = own_heads
                for i, heads in tasks:
                    n = (i + 1) * P
                    ps = score_banks.take()
                    pe.need(un["ready"], ps.free)
                    for j, h in enumerate(heads):
                        out = ps.ap[:, j * n:(j + 1) * n]
                        nc.tensor.matmul(out, q[:, h, i * P:(i + 1) * P], un["K"].ap[:, h, 0:n], start=True, stop=False,
                                         skip_group_check=True)
                    m_cols = min(n, 2 * P)
                    out = ps.ap[:, 0:len(heads) * n].rearrange("p (h n) -> p h n", n=n)[:, :, n - m_cols:n]
                    last = nc.tensor.matmul(out, self.ident16, self.mask_qk[:, 2 * P - m_cols:].unsqueeze(1).to_broadcast(
                        [P, len(heads), m_cols]), start=False, stop=True, skip_group_check=True)
                    dve.need(pe.mark(last))
                    m = dve.mark(nc.vector.tensor_reduce(
                        mx.ap[:, heads[0]:heads[-1] + 1, i:i + 1].rearrange("p h i -> p (h i)"),
                        ps.ap[:, 0:len(heads) * n].rearrange("p (h n) -> p h n", n=n), AXIS, ALU.max))
                    release(ps, m)
                    yield
                for i in (0, 2):
                    ps = score_banks.take()
                    pe.need(un["QN_ready"], st["KB_ready"], ps.free)
                    for j in range(2):
                        last = self.product(ps.ap[:, j * 4 * TC:(j + 1) * 4 * TC], [
                            (un["QN"].ap[:, (i + j) * P:(i + j + 1) * P], st["KB"].ap[:, quad, half].rearrange("p h n -> p (h n)"))
                            for half in range(2)])
                    done = pe.mark(last)
                    dve.need(done)
                    m = dve.mark(nc.vector.tensor_reduce(
                        mx.ap[:, c0:c0 + 4, i:i + 2], ps.ap.rearrange("p (j h n) -> p h j n", h=4, j=2), AXIS, ALU.max))
                    release(ps, m)
                    if i == 0:
                        yield
                yield
                ps = banks.take()
                pe.need(m, ps.free)
                for i in range(NT):
                    last = nc.tensor.transpose(ps.ap[0:4, i * P:(i + 1) * P], mx.ap[:, c0:c0 + 4, i], self.ident)
                done = pe.mark(last)
                if own:
                    ps_own = banks.take()
                    pe.need(ps_own.free)
                    n = own_heads * NT
                    done_own = pe.mark(nc.tensor.transpose(
                        ps_own.ap[0:n, 0:P], mx.ap[:, 0:own_heads, :].rearrange("p h i -> p (h i)"), self.ident))
                    mm = minus_max.take()
                release(mx, (pe.sem, pe.count))
                cm = un["cross_max"] = cross_max.take()
                act.need(done, cm.free)
                m_hi = act.mark(nc.scalar.activation(cm.ap[0:4, :], ps.ap[0:4, :], ACT.Copy, scale=-1.0))
                if own:
                    act.need(done_own, mm.free)
                    m_hi_own = act.mark(nc.scalar.activation(mm.ap[:, 0, :], ps_own.ap[0:n, 0:P], ACT.Copy, scale=-1.0))
                dve.need(m_hi)
                m_lo = dve.mark(nc.vector.scalar_tensor_tensor(
                    out=cm.ap[32:36, :], in0=ps.ap[0:4, :], scalar=-1.0, in1=cm.ap[0:4, :].bitcast(F32),
                    op0=ALU.mult, op1=ALU.subtract))
                release(ps, m_lo)
                un["cross_max_ready"] = [m_hi, m_lo]
                if not own:
                    yield
                    return
                dve.need(m_hi_own)
                m_lo = dve.mark(nc.vector.scalar_tensor_tensor(
                    out=mm.ap[:, 1, :], in0=ps_own.ap[0:n, 0:P], scalar=-1.0, in1=mm.ap[:, 0, :].bitcast(F32),
                    op0=ALU.mult, op1=ALU.subtract))
                release(ps_own, m_lo)
                sp.need(m_lo, (pe.sem, pe.count))
                s = self.stream(f"max{mm.index}")
                for half in range(2):
                    m = s.start(sp, q[ROWS + half:ROWS + half + 1].rearrange("p h (i n) -> p (h i) n", n=P).bitcast(F32),
                                mm.ap[:, half, :].bitcast(F32))
                release(mm, m)
                un["max_ready"] = m
                yield

            def attend(u):
                b, quad = divmod(u, QUADS)
                un, st = unit[u], state[b]
                q = un["Q"].ap if own else None
                vc = st["VC"].ap
                if quad == 0:
                    st["Y"] = Y.take()
                y = st["Y"]
                r = recip.take()

                def exponent(ps, heads, n, done, diagonal):
                    pr = probs.take()
                    act.need(done, pr.free)
                    m = act.mark(nc.scalar.activation(pr.ap[:, 0:heads * n], ps.ap[:, 0:heads * n], ACT.Exp, scale=SCALE))
                    release(ps, m)
                    if diagonal:
                        block = pr.ap[:, 0:heads * n].rearrange("p (h n) -> p h n", n=n)[:, :, 0:P]
                        pool.need(m)
                        m = pool.mark(nc.gpsimd.affine_select(
                            out=block, in_=block, compare_op=ALU.is_ge, fill=0.0, base=0,
                            pattern=[[0, heads], [1, P]], channel_multiplier=-1))
                    return pr, m

                def collected(acc, done):
                    ys = ysum.take()
                    act.need(done, ys.free)
                    m = act.mark(nc.scalar.activation(ys.ap, acc.ap, ACT.Copy))
                    release(acc, m)
                    return ys, m

                def quotient(ys, m, which):
                    ps = banks.take()
                    pe.need(m, ps.free)
                    for i in range(NT):
                        last = nc.tensor.transpose(ps.ap[:, i * P:(i + 1) * P], ys.ap[:, i * P:(i + 1) * P], self.ident)
                    done = pe.mark(last)
                    release(ys, done)
                    v = ps.ap.rearrange("p (i h w) -> p i h w", i=NT, w=VW)
                    dve.need(done, r.free)
                    m = dve.mark(nc.vector.reciprocal(r.ap[:, which], v[:, :, :, DH]))
                    dve.need(m)
                    inv = r.ap[:, which].unsqueeze(3).to_broadcast([P, NT, 4, DH])
                    out = y.ap[:, :, 64 * quad:64 * quad + 64].rearrange("p i (h d) -> p i h d", d=DH)
                    if which == 0:
                        dve.need(y.free)
                        m = dve.mark(nc.vector.tensor_tensor(out, v[:, :, :, 0:DH], inv, ALU.mult))
                    else:
                        m = dve.mark(nc.vector.tensor_tensor(ycross, v[:, :, :, 0:DH], inv, ALU.mult))
                        dve.need(m)
                        m = dve.mark(nc.vector.tensor_tensor(out, out, ycross, ALU.add))
                    release(ps, m)
                    return m

                pieces = {kt: [] for kt in range(NT)}

                def own_scores(kt, h0):
                    n = T - kt * P
                    per = T // n
                    ps = prob_banks.take()
                    pe.need(un["max_ready"], un["ready"], ps.free)
                    for j in range(per):
                        h = h0 + j
                        last = nc.tensor.matmul(ps.ap[:, j * n:(j + 1) * n], un["K"].ap[:, h, kt * P:(kt + 1) * P],
                                                q[:, h, kt * P:T], start=True, stop=True)
                    pieces[kt].append(exponent(ps, per, n, pe.mark(last), True))

                def own_values(kt):
                    n = T - kt * P
                    per = T // n
                    pe.need(st["V_ready"], *[m for _, m in pieces[kt]])
                    if kt == 0:
                        pe.need(acc.free)
                    for h in range(4):
                        pr = pieces[kt][h // per][0]
                        last = nc.tensor.matmul(
                            acc.ap[VW * h:VW * h + VW, kt * P:T], st["V"].ap[:, kt, 4 * quad + h, :],
                            pr.ap[:, (h % per) * n:(h % per + 1) * n], start=kt == 0, stop=kt == NT - 1)
                    done = pe.mark(last)
                    for pr, _ in pieces[kt]:
                        release(pr, done)
                    return done

                crossed = []

                def cross_scores(pair):
                    ps = prob_banks.take()
                    pe.need(un["cross_max_ready"], un["QN_ready"], st["KB_ready"], ps.free)
                    pairs = [(st["KB"].ap[:, quad, half, 2 * pair:2 * pair + 2].rearrange("p h n -> p (h n)"), un["QN"].ap)
                             for half in range(2)]
                    done = pe.mark(self.product(ps.ap, pairs + [(chosen[:, pair, :], un["cross_max"].ap)]))
                    crossed.append(exponent(ps, 1, T, done, False))
                    return done

                if own:
                    acc = value_banks.take()
                    for h in range(4):
                        own_scores(0, h)
                        if h % 2:
                            yield
                    own_scores(1, 0)
                    own_scores(1, 1)
                    yield
                    own_scores(1, 2)
                    own_values(0)
                    yield
                    own_scores(1, 3)
                    own_scores(2, 0)
                    yield
                    own_scores(2, 2)
                    own_values(1)
                    yield
                    own_scores(3, 0)
                    release(un["K"], (pe.sem, pe.count))
                    release(un["Q"], (pe.sem, pe.count))
                    cross_scores(0)
                    yield
                    done = cross_scores(1)
                    own_values(2)
                    release(un["QN"], done)
                    release(un["cross_max"], done)
                    yield
                    done = own_values(3)
                    sums = collected(acc, done)
                    yield
                else:
                    cross_scores(0)
                    done = cross_scores(1)
                    release(un["QN"], done)
                    release(un["cross_max"], done)
                    yield
                acc = value_banks.take()
                pe.need([m for _, m in crossed], st["VC_ready"], acc.free)
                for h in range(4):
                    last = nc.tensor.matmul(acc.ap[VW * h:VW * h + VW, :], vc[:, 4 * quad + h, :],
                                            crossed[h // 2][0].ap, start=True, stop=True)
                done = pe.mark(last)
                for pr, _ in crossed:
                    release(pr, done)
                if quad == QUADS - 1:
                    release(st["KB"], done)
                    release(st["VC"], done)
                    if own:
                        release(st["V"], done)
                if own:
                    quotient(*sums, 0)
                cross_sums = collected(acc, done)
                yield
                m = quotient(*cross_sums, 1 if own else 0)
                release(r, m)
                st["Y_ready"] = m
                yield

            def finish(b):
                st = state[b]
                y = st["Y"]
                xs = residual.take()
                sp.need(st["x_kept"], xs.free)
                x_ready = self.stream("residual").start(sp, xs.ap, x_out[b].rearrange("(t p) c -> p t c", p=P))
                hi, lo = stage.take(), stage.take()
                yT = self.transposed(y.ap, hi.ap, lo.ap, banks, st["Y_ready"], [hi.free, lo.free])
                release(y, (pe.sem, pe.count))
                yield
                halves = {"hi": hi.ap, "lo": lo.ap}
                for half in range(2):
                    ps = banks.take()
                    pe.need(yT, W["o"]["ready"], ps.free)
                    for j in range(2):
                        t = 2 * half + j
                        pairs = [(halves[x][:, kc, t * P:(t + 1) * P], W["o"][a][:, kc, :])
                                 for x, a in (("hi", "hi"), ("lo", "hi"), ("hi", "lo")) for kc in range(CK)]
                        last = self.product(ps.ap[:, j * C:(j + 1) * C], pairs)
                    done = pe.mark(last)
                    dve.need(done, x_ready)
                    two = xs.ap[:, 2 * half:2 * half + 2, :]
                    m = dve.mark(nc.vector.scalar_tensor_tensor(
                        out=two, in0=ps.ap.rearrange("p (t c) -> p t c", t=2), scalar=gate, in1=two, op0=ALU.mult, op1=ALU.add))
                    release(ps, m)
                release(hi, done)
                release(lo, done)
                yield
                sp.need(m)
                m = self.stream(f"x_out{xs.index}").start(sp, x_out[b].rearrange("(t p) c -> p t c", p=P), xs.ap)
                release(xs, m)
                yield

            project, span, behind = (-5.15, 1.0, 1.45) if own else (-4.8, 2.0, 2.3)
            plan = Plan()
            for b in range(B):
                plan.add(QUADS * b + project, 3.8, 12 if own else 8, prepare(b))
                plan.add(QUADS * b + QUADS - 1 + behind + span + 0.2, 1.0, 3, finish(b))
            for u in range(B * QUADS):
                if own:
                    plan.add(u - 0.6, 0.1, 1, pack(u))
                plan.add(u, span, 15 if own else 4, find_max(u))
                plan.add(u + behind, span, 10 if own else 3, attend(u))
            plan.run()
            self.barrier()

    def route_and_share(self, scope, kept):
        nc, pe, act, dve, pool, sp = self.nc, self.pe, self.act, self.dve, self.pool, self.sp
        inp = self.inp
        banks = Ring([self.bank(i) for i in range(4)])
        wide = Ring([self.bank(i) for i in range(4, 8)])
        self.position = self.sb(scope, "position", [P, NTILES], I32)
        self.slot_expert = self.sb(scope, "slot_expert", [1, SLOTS], I32)
        with ExitStack() as mine:
            scaled = self.sb(kept, "m_scaled", [P, NTILES, C])
            tmp = mine.enter_context(Temporary())
            stage = Ring(self.sbs(tmp, "m_wstage", 2, [P, 2 * HID]))
            GW = self.load_split(mine, "m_router", inp["L0_ffn_gate_w"], CK, E, stage)
            SG = self.load_split(mine, "m_sgate", inp["L0_ffn_shared_gate_w"], CK, HID, stage)
            SU = self.load_split(mine, "m_sup", inp["L0_ffn_shared_up_w"], CK, HID, stage)
            SD = self.load_split(mine, "m_sdown", inp["L0_ffn_shared_down_w"], HK, C, stage)
            onehot = self.sb(mine, "m_onehot", [P, NTILES, E])
            prefix = self.sb(mine, "m_prefix", [P, NTILES + 1, E], BF16)
            rank = self.sb(mine, "m_rank", [P, NTILES])
            x_ring = Ring(self.sbs(mine, "m_x", 3, [P, NT, C]))
            xn_ring = Ring(self.sbs(mine, "m_xn", 2, [P, NT, C]))
            stats = self.norm_scratch(mine, "m_ln")
            xT = [Ring(self.sbs(mine, f"m_xT{n}", 2, [P, CK, T], F32R)) for n in ("hi", "lo")]
            hT = [Ring(self.sbs(mine, f"m_hT{n}", 2, [P, HK, T], F32R)) for n in ("hi", "lo")]
            act_out = Ring(self.sbs(mine, "m_silu", 2, [P, T]))
            hidden = Ring(self.sbs(mine, "m_hidden", 2, [P, T]))
            descending = self.sb(mine, "m_descending", [P, E])
            small = {n: self.sb(mine, "m_" + n, [P, NT, E]) for n in ("equal", "first", "work")}
            smallv = {n: self.sb(mine, "m_" + n, [P, NT]) for n in ("top", "best", "score")}
            onehot16 = self.sb(mine, "m_onehot16", [P, NT, E], BF16)
            asc = self.sb(mine, "m_asc", [P, E], I32)
            m = pool.mark(nc.gpsimd.iota(asc, pattern=[[-1, E]], base=E, channel_multiplier=0))
            dve.need(m)
            m1 = dve.mark(nc.vector.tensor_copy(descending, asc))
            m2 = dve.mark(nc.vector.memset(prefix[:, 0, :], 0.0))
            dve.need(m1, m2)
            loaded = {}

            def load(g):
                x = x_ring.take()
                sp.need(x.free)
                loaded[g] = (x, self.stream(f"m_x{x.index}").start(sp, x.ap, self.x1[g].rearrange("(t p) c -> p t c", p=P)))

            keep = {}

            def normalize(g):
                x, m_x = loaded[g]
                xn = xn_ring.take()
                keep[g] = {"xn": xn, "normed": self.norm(x.ap, xn.ap, stats, m_x, xn.free)}

            def transpose(g):
                hi, lo = xT[0].take(), xT[1].take()
                k = keep[g]
                k["ready"] = self.transposed(k["xn"].ap, hi.ap, lo.ap, banks, k["normed"], [hi.free, lo.free])
                k["xT"] = (hi, lo)
                k["xn_read"] = (pe.sem, pe.count)

            def choose(g):
                hi, lo = keep[g]["xT"]
                xn = keep[g]["xn"]
                xh = {"hi": hi.ap, "lo": lo.ap}
                ps = banks.take()
                pe.need(keep[g]["ready"], GW["ready"], ps.free)
                for t in range(NT):
                    pairs = [(xh[a][:, kc, t * P:(t + 1) * P], GW[w][:, kc, :])
                             for a, w in (("hi", "hi"), ("lo", "hi"), ("hi", "lo")) for kc in range(CK)]
                    last = self.product(ps.ap[:, t * E:(t + 1) * E], pairs)
                logits = ps.ap[:, 0:NT * E].rearrange("p (t e) -> p t e", e=E)
                top, best, score = smallv["top"], smallv["best"], smallv["score"]
                eq, first, work = small["equal"], small["first"], small["work"]

                def wide_(v):
                    return v.unsqueeze(2).to_broadcast([P, NT, E])
                dve.need(pe.mark(last), keep.get("score_read"))
                m = dve.mark(nc.vector.tensor_reduce(top, logits, AXIS, ALU.max))
                act.need(m, keep.get("scaled"))
                m_score = act.mark(nc.scalar.activation(score, top, ACT.Sigmoid))
                dve.need(m)
                m = dve.mark(nc.vector.tensor_tensor(eq, logits, wide_(top), ALU.is_equal))
                release(ps, m)
                dve.need(m)
                m = dve.mark(nc.vector.tensor_tensor(first, eq, descending.unsqueeze(1).to_broadcast([P, NT, E]), ALU.mult))
                dve.need(m)
                m = dve.mark(nc.vector.tensor_reduce(best, first, AXIS, ALU.max))
                dve.need(m)
                tiles = slice(g * NT, (g + 1) * NT)
                m = dve.mark(nc.vector.tensor_tensor(onehot[:, tiles, :], first, wide_(best), ALU.is_equal))
                dve.need(m, keep.get("ranked"))
                m_hot = dve.mark(nc.vector.tensor_copy(onehot16, onehot[:, tiles, :]))
                for t in range(NT):
                    n = g * NT + t
                    m = dve.mark(nc.vector.tensor_tensor(prefix[:, n + 1, :], prefix[:, n, :], onehot[:, n, :], ALU.add))
                    dve.need(m)
                keep[g]["chosen"] = [m_hot, m]
                act.need(m_score)
                for t in range(NT):
                    m = act.mark(nc.scalar.activation(scaled[:, g * NT + t, :], xn.ap[:, t, :], ACT.Copy, scale=score[:, t:t + 1]))
                keep["scaled"] = m
                keep["score_read"] = m_score
                release(xn, m, keep[g]["xn_read"])

            def count(g):
                tiles = slice(g * NT, (g + 1) * NT)
                ps = banks.take()
                pe.need(keep[g]["chosen"], ps.free)
                for t in range(NT):
                    out = ps.ap[:, t * E:(t + 1) * E]
                    nc.tensor.matmul(out, self.before, onehot16[:, t, :], start=True, stop=False)
                    last = nc.tensor.matmul(out, self.ones16, prefix[:, g * NT + t, :], start=False, stop=True)
                keep["ranked"] = done = pe.mark(last)
                work = small["work"]
                dve.need(done)
                m = dve.mark(nc.vector.tensor_tensor(work, ps.ap[:, 0:NT * E].rearrange("p (t e) -> p t e", e=E), onehot[:, tiles, :], ALU.mult))
                release(ps, m)
                dve.need(m)
                dve.need(dve.mark(nc.vector.tensor_reduce(rank[:, tiles], work, AXIS, ALU.add)))

            def gate_up(g):
                hi, lo = keep[g]["xT"]
                xh = {"hi": hi.ap, "lo": lo.ap}
                hh, hl = hT[0].take(), hT[1].take()
                keep[g]["hT"] = (hh, hl)
                marks = keep[g]["hidden"] = []
                for mchunk in range(HK):
                    cols = slice(mchunk * P, (mchunk + 1) * P)
                    outs = []
                    for W in (SG, SU):
                        ps = wide.take()
                        pe.need(keep[g]["ready"], W["ready"], ps.free)
                        pairs = [(W[w][:, kc, cols], xh[a][:, kc, :])
                                 for w, a in (("hi", "hi"), ("lo", "hi"), ("hi", "lo")) for kc in range(CK)]
                        outs.append((ps, pe.mark(self.product(ps.ap, pairs))))
                    so, hd = act_out.take(), hidden.take()
                    (pg, mg), (pu, mu) = outs
                    act.need(mg, so.free)
                    m = act.mark(nc.scalar.activation(so.ap, pg.ap, ACT.Silu))
                    release(pg, m)
                    dve.need(m, mu, hd.free)
                    m = dve.mark(nc.vector.tensor_tensor(hd.ap, pu.ap, so.ap, ALU.mult))
                    release(pu, m)
                    release(so, m)
                    act.need(m, hh.free)
                    m1 = act.mark(nc.scalar.activation(hh.ap[:, mchunk, :], hd.ap, ACT.Copy))
                    dve.need(m1, hl.free)
                    m2 = dve.mark(nc.vector.tensor_tensor(hl.ap[:, mchunk, :], hd.ap, hh.ap[:, mchunk, :].bitcast(F32), ALU.subtract))
                    release(hd, m2)
                    marks += [m1, m2]
                    if mchunk == HK - 1:
                        release(hi, (pe.sem, pe.count))
                        release(lo, (pe.sem, pe.count))
                    yield

            def down(g):
                x, _ = loaded[g]
                hh, hl = keep[g]["hT"]
                hs = {"hi": hh.ap, "lo": hl.ap}
                for half in range(2):
                    ps = wide.take()
                    pe.need(keep[g]["hidden"], SD["ready"], ps.free)
                    for j in range(2):
                        t = 2 * half + j
                        pairs = [(hs[a][:, kc, t * P:(t + 1) * P], SD[w][:, kc, :])
                                 for a, w in (("hi", "hi"), ("lo", "hi"), ("hi", "lo")) for kc in range(HK)]
                        last = self.product(ps.ap[:, j * C:(j + 1) * C], pairs)
                    done = pe.mark(last)
                    dve.need(done)
                    two = x.ap[:, 2 * half:2 * half + 2, :]
                    m = dve.mark(nc.vector.scalar_tensor_tensor(
                        out=two, in0=ps.ap.rearrange("p (t c) -> p t c", t=2), scalar=self.gate[:, 2:3], in1=two,
                        op0=ALU.mult, op1=ALU.add))
                    release(ps, m)
                release(hh, done)
                release(hl, done)
                act.need(m)
                m = self.stream(f"m_xo{x.index}").start(act, self.x2[g].rearrange("(t p) c -> p t c", p=P), x.ap)
                release(x, m)

            for g in range(min(B, 3)):
                load(g)
            normalize(0)
            transpose(0)
            choose(0)
            normalize(1)
            for g in range(B):
                chunks = gate_up(g)
                next(chunks)
                count(g)
                next(chunks)
                if g + 1 < B:
                    transpose(g + 1)
                next(chunks)
                next(chunks)
                if g + 1 < B:
                    choose(g + 1)
                if g + 2 < B:
                    normalize(g + 2)
                down(g)
                if g + 3 < B:
                    load(g + 3)
            ps = banks.take()
            pe.need((dve.sem, dve.count), ps.free)
            done = pe.mark(nc.tensor.matmul(ps.ap[:, 0:E], self.ones16, prefix[:, NTILES, :], start=True, stop=True))
            ends = self.sbs(mine, "m_ends", 2, [P, E])
            counts = self.sbs(mine, "m_counts", 2, [P, E], I32)
            slots = self.sb(mine, "m_slots", [P, E])
            first = self.sb(mine, "m_first_row", [P, E])

            def step(instruction):
                m = dve.mark(instruction)
                dve.need(m)
                return m
            dve.need(done)
            step(nc.vector.tensor_scalar(counts[0], ps.ap[:, 0:E], float(P - 1), None, ALU.add))
            step(nc.vector.tensor_scalar(counts[1], counts[0], 7, None, ALU.logical_shift_right))
            step(nc.vector.tensor_copy(slots, counts[1]))
            step(nc.vector.tensor_copy(ends[0], slots))
            cur, shift = 0, 1
            while shift < E:
                a, b = ends[cur], ends[1 - cur]
                step(nc.vector.tensor_copy(b[:, 0:shift], a[:, 0:shift]))
                step(nc.vector.tensor_tensor(b[:, shift:E], a[:, shift:E], a[:, 0:E - shift], ALU.add))
                cur, shift = 1 - cur, 2 * shift
            end = ends[cur]
            step(nc.vector.tensor_tensor(first, end, slots, ALU.subtract))
            step(nc.vector.tensor_scalar(first, first, float(P), None, ALU.mult))
            step(nc.vector.tensor_tensor(onehot, onehot, first.unsqueeze(1).to_broadcast([P, NTILES, E]), ALU.mult))
            base = self.sb(mine, "m_base", [P, NTILES])
            step(nc.vector.tensor_reduce(base, onehot, AXIS, ALU.add))
            step(nc.vector.tensor_tensor(base, base, rank, ALU.add))
            m_pos = step(nc.vector.tensor_copy(self.position, base))
            sl_i = self.sb(mine, "m_sloti", [1, SLOTS], I32)
            sl_f = self.sb(mine, "m_slotf", [1, SLOTS])
            cmp = self.sb(mine, "m_cmp", [1, SLOTS, E])
            cnt = self.sb(mine, "m_cnt", [1, SLOTS])
            dve.need(pool.mark(nc.gpsimd.iota(sl_i, pattern=[[1, SLOTS]], base=0, channel_multiplier=0)))
            step(nc.vector.tensor_copy(sl_f, sl_i))
            step(nc.vector.tensor_tensor(cmp, end[0:1].unsqueeze(1).to_broadcast([1, SLOTS, E]),
                                         sl_f.unsqueeze(2).to_broadcast([1, SLOTS, E]), ALU.is_le))
            step(nc.vector.tensor_reduce(cnt, cmp, AXIS, ALU.add))
            step(nc.vector.tensor_scalar(cnt, cnt, float(E - 1), None, ALU.min))
            step(nc.vector.tensor_copy(self.slot_expert, cnt))
            pool.need(m_pos, (act.sem, act.count), self.stream("zero_sorted").last())
            s = self.stream("scatter")
            for t in range(NTILES):
                nc.gpsimd.indirect_dma_start(
                    out=self.sorted_x[:], out_offset=bass.IndirectOffsetOnAxis(ap=self.position[:, t:t + 1], axis=0),
                    in_=scaled[:, t, :], in_offset=None).then_inc(s.sem, 16)
                s.count += 16
            self.barrier(but=("scatter",))

    def experts(self):
        nc, pe, act, dve, pool, sp = self.nc, self.pe, self.act, self.dve, self.pool, self.sp
        inp = self.inp
        with ExitStack() as scope:
            wg = Ring(self.sbs(scope, "e_gate", 3, [P, CK, HID]))
            wu = Ring(self.sbs(scope, "e_up", 3, [P, CK, HID]))
            wd = Ring(self.sbs(scope, "e_down", 3, [P, HK, C]))
            xr = Ring(self.sbs(scope, "e_x", 3, [P, C]))
            xT = Ring(self.sbs(scope, "e_xT", 2, [P, CK, P]))
            so = Ring(self.sbs(scope, "e_silu", 2, [P, HID]))
            hd = Ring(self.sbs(scope, "e_hidden", 2, [P, HID]))
            hT = Ring(self.sbs(scope, "e_hT", 2, [P, HK, P]))
            yo = Ring(self.sbs(scope, "e_y", 2, [P, C]))
            turn = Ring([self.bank(0), self.bank(1)])
            up = Ring([self.bank(i) for i in (2, 3, 4, 5)])
            down = Ring([self.bank(6), self.bank(7)])
            loads = {}

            def load(j):
                a, b, c, x = wg.take(), wu.take(), wd.take(), xr.take()
                e = sp.q.value_load(self.slot_expert[0:1, j:j + 1], min_val=0, max_val=E - 1)
                sp.need(x.free, self.stream("scatter").last())
                x_ready = self.stream(f"e_x{x.index}").start(sp, x.ap, self.sorted_x[j * P:(j + 1) * P, :])
                marks = []
                for slot, name, tag in ((a, "routed_gate_w", "g"), (b, "routed_up_w", "u"), (c, "routed_down_w", "d")):
                    sp.need(slot.free)
                    marks.append(self.stream(f"e_{tag}{slot.index}").start(
                        sp, slot.ap, inp["L0_ffn_" + name][bass.DynSlice(e, 1)].rearrange("e (c p) n -> p (e c) n", p=P)))
                loads[j] = (a, b, c, x, marks + [x_ready])

            st = {}

            def first(j):
                a, b, c, x, (mg, mu, md, mx) = loads[j]
                ps = turn.take()
                pe.need(mx, ps.free)
                for k in range(CK):
                    last = nc.tensor.transpose(ps.ap[:, k * P:(k + 1) * P], x.ap[:, k * P:(k + 1) * P], self.ident)
                done = pe.mark(last)
                release(x, done)
                t = xT.take()
                act.need(done, t.free)
                m = act.mark(nc.scalar.activation(t.ap, ps.ap[:, 0:C].rearrange("p (c n) -> p c n", c=CK), ACT.Copy))
                release(ps, m)
                st[j] = dict(xT=t, ready=m)

            def second(j):
                a, b, c, x, (mg, mu, md, mx) = loads[j]
                t, m = st[j]["xT"], st[j]["ready"]
                pg, pu = up.take(), up.take()
                pe.need(m, mg, pg.free)
                g = pe.mark(self.product(pg.ap, [(t.ap[:, k, :], a.ap[:, k, :]) for k in range(CK)]))
                pe.need(mu, pu.free)
                u = pe.mark(self.product(pu.ap, [(t.ap[:, k, :], b.ap[:, k, :]) for k in range(CK)]))
                release(a, g)
                release(b, u)
                release(t, u)
                s, h = so.take(), hd.take()
                act.need(g, s.free)
                m = act.mark(nc.scalar.activation(s.ap, pg.ap, ACT.Silu))
                release(pg, m)
                dve.need(m, u, h.free)
                m = dve.mark(nc.vector.tensor_tensor(h.ap, pu.ap, s.ap, ALU.mult))
                release(pu, m)
                release(s, m)
                st[j].update(h=h, h_ready=m)

            def third(j):
                a, b, c, x, (mg, mu, md, mx) = loads[j]
                h = st[j]["h"]
                ps = turn.take()
                pe.need(st[j]["h_ready"], ps.free)
                for k in range(HK):
                    last = nc.tensor.transpose(ps.ap[:, k * P:(k + 1) * P], h.ap[:, k * P:(k + 1) * P], self.ident)
                done = pe.mark(last)
                release(h, done)
                t = hT.take()
                dve.need(done, t.free)
                m = dve.mark(nc.vector.tensor_copy(t.ap, ps.ap.rearrange("p (c n) -> p c n", c=HK)))
                release(ps, m)
                st[j].update(hT=t, hT_ready=m)

            def fourth(j):
                a, b, c, x, (mg, mu, md, mx) = loads[j]
                t = st[j]["hT"]
                ps = down.take()
                pe.need(st[j]["hT_ready"], md, ps.free)
                done = pe.mark(self.product(ps.ap[:, 0:C], [(t.ap[:, k, :], c.ap[:, k, :]) for k in range(HK)]))
                release(c, done)
                release(t, done)
                y = yo.take()
                act.need(done, y.free)
                m = act.mark(nc.scalar.activation(y.ap, ps.ap[:, 0:C], ACT.Copy))
                release(ps, m)
                act.need(m)
                m = self.stream(f"e_y{y.index}").start(act, self.sorted_y[j * P:(j + 1) * P, :], y.ap)
                release(y, m)

            for j in range(-1, SLOTS + 3):
                if j == -1:
                    load(0)
                    load(1)
                    first(0)
                if 0 <= j - 1 < SLOTS:
                    third(j - 1)
                if 0 <= j < SLOTS:
                    second(j)
                if 0 <= j + 1 < SLOTS and j >= 0:
                    first(j + 1)
                if 0 <= j - 1 < SLOTS:
                    fourth(j - 1)
                if 0 <= j and j + 2 < SLOTS:
                    load(j + 2)
            self.barrier()

    def feed_forward(self):
        nc, pe, act, dve, pool, sp = self.nc, self.pe, self.act, self.dve, self.pool, self.sp
        inp = self.inp
        with ExitStack() as scope:
            banks = Ring([self.bank(i) for i in range(8)])
            shapes = dict(w1=(DH1, C), w2=(DH1, C), h1=(DH1, DH1), h2=(DH1, DH1), w3=(C, DH1))
            W, lo_dram, S = {}, {}, {}
            odd = self.sb(scope, "f_odd", [P, 64])
            zeroed = dve.mark(nc.vector.memset(odd, 0.0))
            column = 0
            with Temporary() as tmp:
                rows = Ring(self.sbs(tmp, "f_rows", 3, [P, 4, 512]))
                los = Ring(self.sbs(tmp, "f_los", 8, [P, 512]))
                scr = Slot(self.sb(tmp, "f_scr", [P, 512]), 0)
                pending = []

                def measure(l, lo, ready, stored, column):
                    act.need(ready, zeroed, scr.free)
                    m = act.mark(nc.scalar.activation(scr.ap[:, 0:lo.shape[1]], lo, ACT.Abs, accum_out=odd[:, column:column + 1]))
                    release(scr, m)
                    release(l, m, stored)

                for name, (o, i) in shapes.items():
                    W[name] = hi = self.sb(scope, f"f_{name}", [P, i // P, o], F32R)
                    lo_dram[name] = nc.dram_tensor(f"f_{name}_lo", [P, i // P, o], F32).ap()
                    per_i = min(i, 512)
                    per_o = min(o, 512)
                    for o0 in range(0, o, per_o):
                        for i0 in range(0, i, per_i):
                            nb = per_o // P
                            r = rows.take()
                            sp.need(r.free)
                            m = self.stream(f"f_rows{r.index}").start(
                                sp, r.ap[:, 0:nb, 0:per_i], inp[f"L1_ffn_{name}_w"][o0:o0 + per_o, i0:i0 + per_i].rearrange("(t p) i -> p t i", p=P))
                            for c in range(per_i // P):
                                ps = banks.take()
                                pe.need(m, ps.free)
                                for t in range(nb):
                                    last = nc.tensor.transpose(ps.ap[:, t * P:(t + 1) * P], r.ap[:, t, c * P:(c + 1) * P], self.ident)
                                done = pe.mark(last)
                                src = ps.ap[:, 0:per_o]
                                dst = hi[:, i0 // P + c, o0:o0 + per_o]
                                l = los.take()
                                lo = l.ap[:, 0:per_o]
                                ms = self.split_psum(src, dst, lo, done, l.free)
                                release(ps, *ms)
                                pool.need(ms)
                                md = self.stream(f"f_lo{l.index}").start(pool, lo_dram[name][:, i0 // P + c, o0:o0 + per_o], lo)
                                if pending:
                                    measure(*pending.pop())
                                pending.append((l, lo, ms, md, column))
                                column += 1
                            release(r, done)
                measure(*pending.pop())
                self.barrier()
            ps = banks.take()
            pe.need(ps.free)
            total = self.sb(scope, "f_total", [P, 1])
            flag = self.sb(scope, "f_flag", [1, 1], I32)
            m = dve.mark(nc.vector.tensor_reduce(total, odd, AXIS, ALU.add))
            pe.need(m)
            done = pe.mark(nc.tensor.matmul(ps.ap[0:1, 0:1], total, self.ones[:, 0:1], start=True, stop=True))
            dve.need(done)
            m = dve.mark(nc.vector.tensor_scalar(flag, ps.ap[0:1, 0:1], 0.0, None, ALU.not_equal))
            release(ps, m)
            pe.need(m)
            sp.need(m)
            wider = nc.values_load(flag[0:1, 0:1], engines=[mybir.EngineType.SP, mybir.EngineType.PE], min_val=0, max_val=1)

            for name in ("w1", "w2", "h1", "h2"):
                S[name] = self.sb(scope, f"f_s_{name}", [P, DK])
                m = self.stream("f_scales").start(sp, S[name], inp[f"L1_ffn_{name}_s"].rearrange("(c p) -> p c", p=P), allow_slow_non_contiguous=True)
            s3, m3 = self.load_row(scope, "f_s3", inp["L1_ffn_w3_s"])
            dve.need(m3)
            m3 = dve.mark(nc.vector.tensor_scalar(s3, s3, self.gate[:, 3:4], None, ALU.mult))
            for e in self.engines:
                e.need(m, m3)

            x_ring = Ring(self.sbs(scope, "f_x", 2, [P, NT, C]))
            xn = self.sb(scope, "f_xn", [P, NT, C])
            stats = self.norm_scratch(scope, "f_ln")
            xT = [Ring(self.sbs(scope, f"f_xT{n}", 1, [P, CK, T], F32R)) for n in ("hi", "lo")]
            hs = [Ring(self.sbs(scope, f"f_h{n}", 2, [P, DK, T], F32R)) for n in ("hi", "lo")]
            work = Ring(self.sbs(scope, "f_work", 2, [P, T]))
            lows = Ring(self.sbs(scope, "f_lows", 2, [P, DK, P], F32R))
            self.low_n = 0

            def low_products(name, columns, products):
                n_in = shapes[name][1] // P
                slots = [lows.take() for _ in columns]
                streams = [self.stream(f"f_low{low.index}") for low in slots]
                for low, stream in zip(slots, streams):
                    sp.need(low.free)
                    stream.count += 16
                with nc.If(wider != 0):
                    for low, stream, cols in zip(slots, streams, columns):
                        sp.q.dma_start(low.ap[:, 0:n_in, :].bitcast(F32), lo_dram[name][:, :, cols]).then_inc(stream.sem, 16)
                        pe.q.wait_ge(stream.sem, stream.count)
                    products([low.ap for low in slots])
                with nc.Else():
                    for stream in streams:
                        sp.q.sem_inc(stream.sem, 16)
                return slots

            def linear_T(name, m, src, ready, ps):
                cols = slice(m * P, (m + 1) * P)
                n_in = shapes[name][1] // P
                w = W[name]
                pe.need(ps.free)
                for x in range(2):
                    for k in range(n_in - 1):
                        pe.need(ready[k][x])
                        nc.tensor.matmul(ps.ap, w[:, k, cols], src[x][:, k, :], start=x == 0 and k == 0, stop=False)
                k = n_in - 1
                pe.need(ready[k][0])
                nc.tensor.matmul(ps.ap, w[:, k, cols], src[0][:, k, :], start=False, stop=False)
                slots = low_products(name, [cols], lambda low: self.product(
                    ps.ap, [(low[0][:, k, :], src[0][:, k, :]) for k in range(n_in)], start=False, stop=False))
                pe.need(ready[k][1])
                done = pe.mark(nc.tensor.matmul(ps.ap, w[:, k, cols], src[1][:, k, :], start=False, stop=True))
                for low in slots:
                    release(low, done)
                return done

            loaded, keep = {}, {}

            def load(g):
                x = x_ring.take()
                sp.need(x.free)
                loaded[g] = (x, self.stream(f"f_x{x.index}").start(sp, x.ap, self.x3[g].rearrange("(t p) c -> p t c", p=P)))

            def normalize(g):
                x, m_x = loaded[g]
                keep["normed"] = self.norm(x.ap, xn, stats, m_x, keep.get("xn_free"))

            def prepare(g):
                hi, lo = xT[0].take(), xT[1].take()
                ready = self.transposed(xn, hi.ap, lo.ap, banks, keep["normed"], [hi.free, lo.free])
                keep["xn_free"] = [(pe.sem, pe.count)]
                keep[g] = (hi, lo, list(zip(ready[0::2], ready[1::2])))

            def group(g):
                x_slot, _ = loaded[g]
                hi, lo, ready = keep[g]
                src, src_slots = (hi.ap, lo.ap), (hi, lo)
                out = (hs[0].take(), hs[1].take())
                marks = []
                for m in range(DK):
                    pa, pb = banks.take(), banks.take()
                    da = linear_T("w1", m, src, ready, pa)
                    db = linear_T("w2", m, src, ready, pb)
                    w = work.take()
                    act.need(da, w.free)
                    ms = act.mark(nc.scalar.activation(w.ap, pa.ap, ACT.Silu, scale=S["w1"][:, m:m + 1]))
                    release(pa, ms)
                    dve.need(ms, db)
                    mh = dve.mark(nc.vector.scalar_tensor_tensor(out=w.ap, in0=pb.ap, scalar=S["w2"][:, m:m + 1], in1=w.ap,
                                                                 op0=ALU.mult, op1=ALU.mult))
                    release(pb, mh)
                    act.need(mh, out[0].free)
                    m1 = act.mark(nc.scalar.activation(out[0].ap[:, m, :], w.ap, ACT.Copy))
                    dve.need(m1, out[1].free)
                    m2 = dve.mark(nc.vector.tensor_tensor(out[1].ap[:, m, :], w.ap, out[0].ap[:, m, :].bitcast(F32), ALU.subtract))
                    release(w, m2)
                    marks.append((m1, m2))
                for s in src_slots:
                    release(s, (pe.sem, pe.count))
                if g + 1 < B:
                    normalize(g + 1)
                for name in ("h1", "h2"):
                    src, src_slots, ready = (out[0].ap, out[1].ap), out, marks
                    out = (hs[0].take(), hs[1].take())
                    marks = []
                    for m in range(DK):
                        ps = banks.take()
                        done = linear_T(name, m, src, ready, ps)
                        w = work.take()
                        act.need(done, w.free)
                        ms = act.mark(nc.scalar.activation(w.ap, ps.ap, ACT.Gelu, scale=S[name][:, m:m + 1]))
                        release(ps, ms)
                        dve.need(ms, out[0].free, out[1].free)
                        m1 = dve.mark(nc.vector.tensor_copy(out[0].ap[:, m, :], w.ap))
                        dve.need(m1)
                        m2 = dve.mark(nc.vector.tensor_tensor(out[1].ap[:, m, :], w.ap, out[0].ap[:, m, :].bitcast(F32), ALU.subtract))
                        release(w, m2)
                        marks.append((m1, m2))
                    for s in src_slots:
                        release(s, (pe.sem, pe.count))
                    if name == "h1" and g + 1 < B:
                        prepare(g + 1)
                src = (out[0].ap, out[1].ap)
                w = W["w3"]
                for pair in range(NT // 2):
                    ps = banks.take()
                    pe.need(ps.free)
                    tiles = [(ps.ap[:, j * C:(j + 1) * C], slice((2 * pair + j) * P, (2 * pair + j + 1) * P)) for j in range(2)]
                    for x in range(2):
                        for k in range(DK - x):
                            pe.need(marks[k][x])
                            for j, (o, toks) in enumerate(tiles):
                                nc.tensor.matmul(o, src[x][:, k, toks], w[:, k, :], start=x == 0 and k == 0 and j == 0,
                                                 stop=False, skip_group_check=True)

                    def third(low):
                        for o, toks in tiles:
                            for half in range(CK):
                                self.product(o[:, half * P:(half + 1) * P], [(src[0][:, k, toks], low[half][:, k, :]) for k in range(DK)],
                                             start=False, stop=False, skip_group_check=True)
                    slots = low_products("w3", [slice(0, P), slice(P, 2 * P)], third)
                    pe.need(marks[DK - 1][1])
                    for o, toks in tiles:
                        last = nc.tensor.matmul(o, src[1][:, DK - 1, toks], w[:, DK - 1, :], start=False, stop=True, skip_group_check=True)
                    done = pe.mark(last)
                    for low in slots:
                        release(low, done)
                    wk = work.take()
                    dve.need(done, wk.free)
                    v = wk.ap.rearrange("p (t c) -> p t c", t=2)
                    m = dve.mark(nc.vector.tensor_tensor(v, ps.ap.rearrange("p (t c) -> p t c", t=2),
                                                         s3.unsqueeze(1).to_broadcast([P, 2, C]), ALU.mult))
                    release(ps, m)
                    pool.need(m)
                    part = x_slot.ap[:, 2 * pair:2 * pair + 2, :]
                    m = pool.mark(nc.gpsimd.tensor_tensor(part, part, v, ALU.add))
                    release(wk, m)
                for s in out:
                    release(s, done)
                sp.need(m)
                m = self.stream(f"f_out{x_slot.index}").start(sp, self.out[g].rearrange("(t p) c -> p t c", p=P), x_slot.ap)
                release(x_slot, m)
                if g + 2 < B:
                    load(g + 2)

            load(0)
            load(1)
            normalize(0)
            prepare(0)
            for g in range(B):
                group(g)
            self.barrier()

    def build(self):
        with ExitStack() as scope:
            self.constants(scope)
            with ExitStack() as weights:
                self.attention(0, *self.attention_weights(0, weights))
            with ExitStack() as weights:
                with Temporary() as kept:
                    self.route_and_share(scope, kept)
                    prepared = self.attention_weights(1, weights)
                    self.experts()
                self.attention(1, *prepared)
            self.feed_forward()
            self.barrier()


def kernel(**inputs):
    import numpy as np
    import concourse.bacc as bacc
    from concourse.bass_utils import run_bass_kernel_spmd

    nc = bacc.Bacc("TRN2", target_bir_lowering=False, num_devices=1)
    arrays, args = {}, {}
    for name, value in inputs.items():
        a = np.ascontiguousarray(value)
        arrays[f"in_{name}"] = a
        args[name] = nc.dram_tensor(f"in_{name}", a.shape, mybir.dt.from_np(a.dtype), kind="ExternalInput").ap()
    out = nc.dram_tensor("out_x", (B, T, C), F32, kind="ExternalOutput").ap()
    Program(nc, args, out).build()
    r = run_bass_kernel_spmd(nc, [arrays], core_ids=[0])
    return r.results[0]["out_x"]
```
